# Optimizing a Trainium2 kernel written in Bass

```python
import numpy as np
import jax
import jax.numpy as jnp

def _softmax(x, axis=-1):
    return jax.nn.softmax(x, axis=axis)

def _gelu(x):
    return jax.nn.gelu(x, approximate=True)

def _silu(x):
    return jax.nn.silu(x)

def _sigmoid(x):
    return jax.nn.sigmoid(x)

def _layernorm(x, axis=-1, eps=1e-05):
    m = jnp.mean(x, axis=axis, keepdims=True)
    v = jnp.var(x, axis=axis, keepdims=True)
    return (x - m) / jnp.sqrt(v + eps)

def _scatter_add(tgt, idx, src, axis=0):
    return tgt.at[idx].add(src)

def _segment_sum(src, seg, n):
    return jax.ops.segment_sum(src, seg, n)
kernel_name = 'mk_xattn_ffn_d1_seqx_r8_f02107'

def setup_inputs(seed: int=0):
    np.random.seed(seed)
    _w = jnp.asarray

    def _rec_inputs():
        import jax
        import jax.numpy as jnp
        _rk = jax.random.key(seed)
        x = 0.0001212 + 1 * jax.random.normal(jax.random.fold_in(_rk, 1), (128, 64, 128), jnp.float32)
        _lenS = 64 - jax.random.randint(jax.random.fold_in(_rk, 7), (128,), 0, max(1, 64 // 4) + 1, jnp.int32)
        _lenS2 = 64 - jax.random.randint(jax.random.fold_in(_rk, 8), (128,), 0, max(1, 64 // 4) + 1, jnp.int32)
        _ctx_1024P = jax.random.normal(jax.random.fold_in(_rk, 11), (128, 16, 128), jnp.float32)
        _ctx_1024c = jax.random.dirichlet(jax.random.fold_in(_rk, 511), 0.3 * jnp.ones((16,), jnp.float32), (128, 64))
        _ctx_1024t = jnp.einsum('bsk,bkd->bsd', _ctx_1024c, _ctx_1024P)
        _ctx_1024t = _ctx_1024t * jax.lax.rsqrt(jnp.mean(jnp.square(_ctx_1024t)) + 1e-12) * 0.953939
        ctx_1024 = -0.000125008 + 0.999885 * (_ctx_1024t + 0.3 * jax.random.normal(jax.random.fold_in(_rk, 611), (128, 64, 128), jnp.float32))
        return (x, ctx_1024)
    x, ctx_1024 = _rec_inputs()

    def _L0_xattn_setup():
        import jax, jax.numpy as jnp
        import numpy as np
        B, L, D_MODEL, N_HEADS = (4, 1024, 128, 16)
        D_DEPTH = D_MODEL // N_HEADS

        def _split_heads(x):
            b, l, _ = x.shape
            return x.reshape(b, l, N_HEADS, D_DEPTH).transpose(0, 2, 1, 3)

        def _combine_heads(x):
            b, _, l, _ = x.shape
            return x.transpose(0, 2, 1, 3).reshape(b, l, D_MODEL)
        key = jax.random.key(seed)
        ks = jax.random.split(key, 8)
        s = 1.0 / np.sqrt(D_MODEL)
        return {'v': jax.random.normal(ks[0], (B, L, D_MODEL), dtype=jnp.float32), 'k': jax.random.normal(ks[1], (B, L, D_MODEL), dtype=jnp.float32), 'q': jax.random.normal(ks[2], (B, L, D_MODEL), dtype=jnp.float32), 'wq_w': jax.random.normal(ks[3], (D_MODEL, D_MODEL), dtype=jnp.float32) * s, 'wq_b': jnp.zeros((D_MODEL,), jnp.float32), 'wk_w': jax.random.normal(ks[4], (D_MODEL, D_MODEL), dtype=jnp.float32) * s, 'wk_b': jnp.zeros((D_MODEL,), jnp.float32), 'wv_w': jax.random.normal(ks[5], (D_MODEL, D_MODEL), dtype=jnp.float32) * s, 'wv_b': jnp.zeros((D_MODEL,), jnp.float32), 'wc_w': jax.random.normal(ks[6], (D_MODEL, D_MODEL), dtype=jnp.float32) * s, 'wc_b': jnp.zeros((D_MODEL,), jnp.float32)}
    _L0_xattn_all = _L0_xattn_setup()
    _L0_xattn_in = {k: v for k, v in _L0_xattn_all.items() if k in ('wq_w', 'wq_b', 'wk_w', 'wk_b', 'wv_w', 'wv_b', 'wc_w', 'wc_b')}
    del _L0_xattn_all

    def _L0_ffn_setup():
        import jax, jax.numpy as jnp
        import numpy as np
        D, H, O, E, TOPK = (128, 512, 128, 8, 2)
        B, S = (4, 128)
        key = jax.random.key(seed)
        ks = jax.random.split(key, 12)
        std = 0.02
        return {'hidden_states': jax.random.normal(ks[0], (B, S, D), dtype=jnp.float32), 'norm_weight': jnp.ones((D,), dtype=jnp.float32), 'router_w': jax.random.normal(ks[1], (E, D), dtype=jnp.float32) * std, 'sw1': jax.random.normal(ks[2], (D, H), dtype=jnp.float32) * (1.0 / np.sqrt(D)), 'sb1': jnp.zeros((H,), dtype=jnp.float32), 'sw2': jax.random.normal(ks[3], (H, O), dtype=jnp.float32) * (1.0 / np.sqrt(H)), 'sb2': jnp.zeros((O,), dtype=jnp.float32), 'ew1': jax.random.normal(ks[4], (E, D, H), dtype=jnp.float32) * (1.0 / np.sqrt(D)), 'eb1': jnp.zeros((E, H), dtype=jnp.float32), 'ew2': jax.random.normal(ks[5], (E, H, O), dtype=jnp.float32) * (1.0 / np.sqrt(H)), 'eb2': jnp.zeros((E, O), dtype=jnp.float32)}
    _L0_ffn_all = _L0_ffn_setup()
    _L0_ffn_in = {k: v for k, v in _L0_ffn_all.items() if k in ('norm_weight', 'router_w', 'sw1', 'sb1', 'sw2', 'sb2', 'ew1', 'eb1', 'ew2', 'eb2')}
    del _L0_ffn_all
    return {'x': x, 'ctx_1024': ctx_1024, 'L0_xattn_wq_w': _L0_xattn_in['wq_w'], 'L0_xattn_wq_b': _L0_xattn_in['wq_b'], 'L0_xattn_wk_w': _L0_xattn_in['wk_w'], 'L0_xattn_wk_b': _L0_xattn_in['wk_b'], 'L0_xattn_wv_w': _L0_xattn_in['wv_w'], 'L0_xattn_wv_b': _L0_xattn_in['wv_b'], 'L0_xattn_wc_w': _L0_xattn_in['wc_w'], 'L0_xattn_wc_b': _L0_xattn_in['wc_b'], 'L0_ffn_norm_weight': _L0_ffn_in['norm_weight'], 'L0_ffn_router_w': _L0_ffn_in['router_w'], 'L0_ffn_sw1': _L0_ffn_in['sw1'], 'L0_ffn_sb1': _L0_ffn_in['sb1'], 'L0_ffn_sw2': _L0_ffn_in['sw2'], 'L0_ffn_sb2': _L0_ffn_in['sb2'], 'L0_ffn_ew1': _L0_ffn_in['ew1'], 'L0_ffn_eb1': _L0_ffn_in['eb1'], 'L0_ffn_ew2': _L0_ffn_in['ew2'], 'L0_ffn_eb2': _L0_ffn_in['eb2']}

def reference(x, ctx_1024, L0_xattn_wq_w, L0_xattn_wq_b, L0_xattn_wk_w, L0_xattn_wk_b, L0_xattn_wv_w, L0_xattn_wv_b, L0_xattn_wc_w, L0_xattn_wc_b, L0_ffn_norm_weight, L0_ffn_router_w, L0_ffn_sw1, L0_ffn_sb1, L0_ffn_sw2, L0_ffn_sb2, L0_ffn_ew1, L0_ffn_eb1, L0_ffn_ew2, L0_ffn_eb2):
    import jax
    import jax.numpy as jnp

    def _L0_xattn_ref(v, k, q, wq_w, wq_b, wk_w, wk_b, wv_w, wv_b, wc_w, wc_b):
        import jax, jax.numpy as jnp
        import numpy as np
        B, L, D_MODEL, N_HEADS = (4, 1024, 128, 16)
        D_DEPTH = D_MODEL // N_HEADS

        def _split_heads(x):
            b, l, _ = x.shape
            return x.reshape(b, l, N_HEADS, D_DEPTH).transpose(0, 2, 1, 3)

        def _combine_heads(x):
            b, _, l, _ = x.shape
            return x.transpose(0, 2, 1, 3).reshape(b, l, D_MODEL)
        q_heads = jax.nn.elu(_split_heads(q @ wq_w + wq_b)) + 1.0
        k_heads = jax.nn.elu(_split_heads(k @ wk_w + wk_b)) + 1.0
        v_heads = _split_heads(v @ wv_w + wv_b)
        k_cumsum = jnp.cumsum(k_heads, axis=1)
        attn_free = q_heads * (k_heads / k_cumsum) * v_heads
        return _combine_heads(attn_free) @ wc_w + wc_b

    def _L0_ffn_ref(hidden_states, norm_weight, router_w, sw1, sb1, sw2, sb2, ew1, eb1, ew2, eb2):
        import jax, jax.numpy as jnp
        import numpy as np
        D, H, O, E, TOPK = (128, 512, 128, 8, 2)
        B, S = (4, 128)
        b, s, d = hidden_states.shape
        var = jnp.mean(jnp.square(hidden_states), axis=-1, keepdims=True)
        normed = hidden_states * jax.lax.rsqrt(var + 1e-08) * norm_weight
        shared = jnp.maximum(normed @ sw1 + sb1, 0.0) @ sw2 + sb2
        flat = normed.reshape(-1, d)
        T = flat.shape[0]
        probs = jax.nn.sigmoid(flat @ router_w.T)
        scores, idx = jax.lax.top_k(probs, TOPK)
        w = scores / (jnp.sum(scores, axis=-1, keepdims=True) + 1e-06)
        comb = jnp.zeros((T, E), dtype=flat.dtype)
        comb = comb.at[jnp.arange(T)[:, None], idx].add(w)
        h = jnp.maximum(jnp.einsum('td,edh->teh', flat, ew1) + eb1[None, :, :], 0.0)
        eo = jnp.einsum('teh,eho->teo', h, ew2) + eb2[None, :, :]
        routed = jnp.einsum('teo,te->to', eo, comb)
        return shared + routed.reshape(b, s, -1)
    x = x + _L0_xattn_ref(ctx_1024, ctx_1024, _layernorm(x, axis=-1), L0_xattn_wq_w, L0_xattn_wq_b, L0_xattn_wk_w, L0_xattn_wk_b, L0_xattn_wv_w, L0_xattn_wv_b, L0_xattn_wc_w, L0_xattn_wc_b)
    x = x + _L0_ffn_ref(_layernorm(x, axis=-1), L0_ffn_norm_weight, L0_ffn_router_w, L0_ffn_sw1, L0_ffn_sb1, L0_ffn_sw2, L0_ffn_sb2, L0_ffn_ew1, L0_ffn_eb1, L0_ffn_ew2, L0_ffn_eb2)
    return x

_drawn_inputs = setup_inputs


def setup_inputs(seed=0):
    import zlib

    import numpy as np

    out = dict(_drawn_inputs(seed))
    spreads = {'L0_xattn_wq_b': (0.0, 0.1),
     'L0_xattn_wk_b': (0.0, 0.1),
     'L0_xattn_wv_b': (0.0, 0.1),
     'L0_xattn_wc_b': (0.0, 0.1),
     'L0_ffn_norm_weight': (1.0, 0.2),
     'L0_ffn_sb1': (0.0, 0.1),
     'L0_ffn_sb2': (0.0, 0.1),
     'L0_ffn_eb1': (0.0, 0.1),
     'L0_ffn_eb2': (0.0, 0.1)}
    factors = {}
    for name, (base, spread) in spreads.items():
        noise = np.random.default_rng([zlib.crc32(name.encode()), seed]).standard_normal(out[name].shape)
        drawn = base * np.exp(spread * noise) if base else spread * noise
        out[name] = jnp.asarray(drawn.astype(out[name].dtype))
    for name, factor in factors.items():
        out[name] = (out[name] * factor).astype(out[name].dtype)
    return out
```

```python
from contextlib import ExitStack

import numpy as np

import concourse.bass as bass
from concourse import mybir

F32 = mybir.dt.float32
I32 = mybir.dt.int32
ALU = mybir.AluOpType
ACT = mybir.ActivationFunctionType
AX = mybir.AxisListType.X

P = 128
D = 128
HID = 512
HC = HID // P
E = 8
TOPK = 2
HEADS, DEPTH = 16, 8
TOKENS = 128 * 64
SUB = 4
TILE = P * SUB
TILES = TOKENS // TILE
LN_EPS = 1e-5
RMS_EPS = 1e-8
COMB_EPS = 1e-6
SIG_ONE, SIG_ZERO = 16.635532, -88.0

COL_W, COL_ID, ROW = D, D + E, 140
REGION = TOKENS + TILE
PAD_ROW = E * REGION
X_ROWS = PAD_ROW + TILE
XTILES = TOPK * TOKENS // TILE + E - 1
OUT_ROWS = TOKENS + TILE
COL_B1, COL_B2, COL_HOT, EXTRA = 0, HC, HC + 1, HC + 1 + E
CM_IDENT, CM_BEFORE, CM_ONES, CM_HEADS = 0, P, 2 * P, 3 * P
CS_BASE, CS_ORDER, CS_ID = 4 * P, 4 * P + SUB * E, 4 * P + 2 * SUB * E
CONSTS = CS_ID + SUB
TB_STEP, TB_UPTO, TB_TILE, TB_REG = 0, E * TILES, E * TILES + E * E, E * TILES + E * E + XTILES
TABLES = TB_REG + E
V_BQ, V_BK, V_BV, V_BC, V_NW, V_SB1, V_SB2 = 0, 1, 2, 3, 4, 5, 5 + HC
VECS = V_SB2 + 1


def constants():
    c = np.zeros((P, CONSTS), np.float32)
    i = np.arange(P)
    c[:, CM_IDENT:CM_IDENT + P] = np.eye(P)
    c[:, CM_BEFORE:CM_BEFORE + P] = i[:, None] < i[None, :]
    c[:, CM_ONES:CM_ONES + P] = 1
    same_place = i[:, None] % DEPTH == i[None, :] % DEPTH
    c[:, CM_HEADS:CM_HEADS + P] = same_place & (i[:, None] // DEPTH <= i[None, :] // DEPTH)
    c[:, CS_BASE:CS_BASE + SUB * E] = np.tile(np.arange(E) * REGION, SUB)
    c[:, CS_ORDER:CS_ORDER + SUB * E] = np.tile(E - np.arange(E), SUB)
    c[:, CS_ID:CS_ID + SUB] = np.arange(TILE).reshape(P, SUB)
    t = np.zeros((1, TABLES), np.float32)
    t[0, TB_STEP:TB_UPTO] = np.tile(np.arange(TILES) * TILE, E)
    t[0, TB_UPTO:TB_TILE] = (np.arange(E)[None, :] <= np.arange(E)[:, None]).ravel()
    t[0, TB_TILE:TB_REG] = np.arange(XTILES)
    t[0, TB_REG:] = np.arange(E) * REGION
    return c, t


class Tile:

    def __init__(self, pair, offset):
        self.par = offset % 2
        self.half = pair + offset // 2
        self.n = 2 * pair + offset if isinstance(pair, int) else pair * 2 + offset
        self.static = isinstance(pair, int)
        self.pair, self.offset = pair, offset

    def later(self, k):
        return Tile(self.pair, self.offset + k)

    def at_least(self, k):
        return not self.static or self.n >= k

    def exists(self):
        return not self.static or 0 <= self.n < TILES


def token_kernel(nc, x, ctx_in, wq, wk, wv, wc, vecs, router, sw1, sw2, ew1, ew2, extra, consts, tables,
                 rows_dram, out):
    with ExitStack() as stack:
        def sb(name, shape, dt=F32):
            return stack.enter_context(nc.sbuf_tensor("sb_" + name, shape, dt))

        def bank(name):
            return stack.enter_context(nc.psum_tensor("ps_" + name, [P, TILE], F32))

        def sem(name):
            return stack.enter_context(nc.semaphore(name))

        def pair_of(make, name):
            return [make(f"{name}{k}") for k in range(2)]

        cst = sb("cst", [P, CONSTS])
        tab = sb("tab", [1, TABLES])
        vec = sb("vec", [P, VECS])
        w_q, w_k, w_v, w_c = (sb(n, [P, D]) for n in ("w_q", "w_k", "w_v", "w_c"))
        w_r = sb("w_r", [P, E])
        w_s1 = sb("w_s1", [P, HID])
        w_s2 = sb("w_s2", [P, HC, D])
        x_sb = [sb(f"x{k}", [P, SUB, D]) for k in range(2)]
        c_sb = [sb(f"c{k}", [P, SUB, D]) for k in range(2)]
        xn = sb("xn", [P, SUB, D])
        xnT, ctxT = sb("xnT", [P, TILE]), sb("ctxT", [P, TILE])
        k_exp, k_lin, q_exp, q_lin = (sb(n, [P, TILE]) for n in ("k_exp", "k_lin", "q_exp", "q_lin"))
        kT, qT = sb("kT", [P, TILE]), sb("qT", [P, TILE])
        k_inv, qk, qkn, attnT = (sb(n, [P, TILE]) for n in ("k_inv", "qk", "qkn", "attnT"))
        projT = sb("projT", [P, TILE])
        x2 = sb("x2", [P, SUB, D])
        rows = [sb(f"rows{k}", [P, SUB, ROW]) for k in range(2)]
        nT = sb("nT", [P, TILE])
        hT = sb("hT", [P, HC, TILE])
        yT = sb("yT", [P, TILE])
        out_sb = [sb(f"out{k}", [P, SUB, D]) for k in range(2)]
        pad = sb("pad", [P, SUB, ROW])
        st = [sb(f"st{k}", [P, SUB, 6]) for k in range(2)]
        mv = [sb(f"mv{k}", [P, SUB, 2]) for k in range(2)]
        spread = [sb(f"spread{k}", [P, SUB]) for k in range(2)]
        neg_mean = [sb(f"neg_mean{k}", [P, SUB]) for k in range(2)]
        rstd = [sb(f"rstd{k}", [P, SUB]) for k in range(2)]
        shift = [sb(f"shift{k}", [P, SUB]) for k in range(2)]
        carried = sb("carried", [P, 2])
        minus_half = sb("minus_half", [P, SUB])
        key, key2, e_neg, den, prob = (sb(n, [P, SUB, E]) for n in ("key", "key2", "e_neg", "den", "prob"))
        best = sb("best", [P, SUB])
        hit = sb("hit", [P, SUB, E])
        ranked = sb("ranked", [P, SUB, E])
        hot = sb("hot", [P, TOPK, SUB, E])
        chosen = sb("chosen", [P, SUB, E])
        score = sb("score", [P, SUB, E])
        total, inv_total = sb("total", [P, SUB]), sb("inv_total", [P, SUB])
        seen = sb("seen", [P, SUB + 1, E])
        place = sb("place", [P, SUB, E])
        placed = sb("placed", [P, TOPK, SUB, E])
        slot_f = sb("slot_f", [P, TOPK, SUB])
        slot = [sb(f"slot{k}", [P, TOPK, SUB], I32) for k in range(2)]
        cnt = sb("cnt", [1, E])
        tl_a, tl_n = sb("tl_a", [1, E, TILES]), sb("tl_n", [1, E])
        tl_b, tl_end = sb("tl_b", [1, E, E]), sb("tl_end", [1, E])
        tl_past, tl_used = sb("tl_past", [1, XTILES, E]), sb("tl_used", [1, XTILES, E])
        tl_e, tl_first = sb("tl_e", [1, XTILES]), sb("tl_first", [1, XTILES])
        tl_k, tl_base, tl_row = (sb(n, [1, XTILES]) for n in ("tl_k", "tl_base", "tl_row"))
        row_of, expert_of = sb("row_of", [1, XTILES], I32), sb("expert_of", [1, XTILES], I32)
        pad_at = sb("pad_at", [1, E], I32)
        DEEP = 3
        xb = [sb(f"xb{k}", [P, SUB, ROW]) for k in range(DEEP)]
        w1b = [sb(f"w1b{k}", [P, HID]) for k in range(DEEP)]
        w2b = [sb(f"w2b{k}", [P, HC, D]) for k in range(DEEP)]
        exb = [sb(f"exb{k}", [P, EXTRA]) for k in range(DEEP)]
        yb = [sb(f"yb{k}", [P, SUB, D]) for k in range(DEEP)]
        tok = [sb(f"tok{k}", [P, SUB], I32) for k in range(DEEP)]
        w_pick, w_row = sb("w_pick", [P, SUB, E]), sb("w_row", [P, SUB])

        b = [bank(f"b{k}") for k in range(8)]
        ps_ctxT, ps_xT, ps_k, ps_v, ps_q, ps_csum = b[0], b[1], b[2], b[3], b[4], b[6]
        ps_projT, ps_proj, ps_nT, ps_yT, ps_y = b[0], b[1], b[5], b[4], b[5]
        ps_h = [b[0], b[1], b[5], b[2]]
        ps_logit, ps_rank, ps_count = b[7][:, 0:SUB * E], b[7][:, 64:64 + SUB * E], b[7][:, 128:128 + E]
        pb_xT, pb_h, pb_yT, pb_y = b[0], b[1:5], b[5], b[6]

        ident, before = cst[:, CM_IDENT:CM_IDENT + P], cst[:, CM_BEFORE:CM_BEFORE + P]
        ones, heads = cst[:, CM_ONES:CM_ONES + P], cst[:, CM_HEADS:CM_HEADS + P]
        base = cst[:, CS_BASE:CS_BASE + SUB * E].rearrange("p (s e) -> p s e", s=SUB)
        order = cst[:, CS_ORDER:CS_ORDER + SUB * E].rearrange("p (s e) -> p s e", s=SUB)
        id0 = cst[:, CS_ID:CS_ID + SUB]

        consts_in = sem("consts_in")
        weights_in = sem("weights_in")
        x_in, c_in = pair_of(sem, "x_in"), pair_of(sem, "c_in")
        setup = sem("setup")
        ctxT_ps, xT_ps, k_ps, v_ps, q_ps = (sem(n) for n in ("ctxT_ps", "xT_ps", "k_ps", "v_ps", "q_ps"))
        csum_ps, projT_ps, proj_ps = sem("csum_ps"), sem("projT_ps"), sem("proj_ps")
        rank_ps, nT_ps, logit_ps = sem("rank_ps"), sem("nT_ps"), sem("logit_ps")
        h_ps, yT_ps, y_ps, count_ps = sem("h_ps"), sem("yT_ps"), sem("y_ps"), sem("count_ps")
        ctxT_sb, k_parts, q_parts = sem("ctxT_sb"), sem("k_parts"), sem("q_parts")
        xn_sb, rows_sb, e_sb = sem("xn_sb"), sem("rows_sb"), sem("e_sb")
        h_sb, yT_sb, projT_sb = sem("h_sb"), sem("yT_sb"), sem("projT_sb")
        xnT_sb, kT_sb, qT_sb, nT_sb = sem("xnT_sb"), sem("kT_sb"), sem("qT_sb"), sem("nT_sb")
        inv_sb, qk_sb, qkn_sb, attn_sb = sem("inv_sb"), sem("qk_sb"), sem("qkn_sb"), sem("attn_sb")
        place_sb, placed_sb, slot_f_sb, slot_sb = (sem(n) for n in ("place_sb", "placed_sb", "slot_f_sb", "slot_sb"))
        key_sb, routed, out_ready, x2_sb = sem("key_sb"), sem("routed"), sem("out_ready"), sem("x2_sb")
        inv_total_sb = sem("inv_total_sb")
        route = sem("route")
        stat = [sem("stat1"), sem("stat2")]
        spread_sb = [sem("spread1"), sem("spread2")]
        power = [sem("power1"), sem("power2")]
        shift_sb = [sem("shift1"), sem("shift2")]
        stored = pair_of(sem, "stored")
        scattered = pair_of(sem, "scattered")
        SCATTERS = TOPK * SUB
        table = sem("table")
        table_done = sem("table_done")
        pads_in = sem("pads_in")
        dummies_in = sem("dummies_in")
        pool_carried = sem("pool_carried")
        xb_in = [sem(f"xb_in{k}") for k in range(DEEP)]
        wb_in = [sem(f"wb_in{k}") for k in range(DEEP)]
        bxT_ps, bh_ps, byT_ps, by_ps = sem("bxT_ps"), sem("bh_ps"), sem("byT_ps"), sem("by_ps")
        bxT_sb, bh_sb, byT_sb, by_sb = sem("bxT_sb"), sem("bh_sb"), sem("byT_sb"), sem("by_sb")
        pick_sb, w_sb = sem("pick_sb"), sem("w_sb")
        added = sem("added")

        x_t = x.rearrange("(t p s) d -> t p (s d)", p=P, s=SUB)
        c_t = ctx_in.rearrange("(t p s) d -> t p (s d)", p=P, s=SUB)
        out_t = out.rearrange("(t p s) d -> t p (s d)", p=P, s=SUB)
        FIRST = Tile(0, 0)
        SCAT_ALL = 16 * SCATTERS * TILES // 2

        def pipeline(engine, step):
            for t in range(4):
                step(Tile(0, t))
            with engine.Fori(2, TILES // 2 - 1) as pair:
                step(Tile(pair, 0))
                step(Tile(pair, 1))
            for t in range(TILES - 2, TILES + 2):
                step(Tile(0, t))

        def experts(engine, step):
            for u in range(DEEP):
                step(0, u)
            with engine.Fori(1, XTILES // DEEP - 1) as i:
                for u in range(DEEP):
                    step(i, u)
            for u in range(DEEP):
                step(XTILES // DEEP - 1, u)

        assert XTILES % DEEP == 0

        def carry_wait_dve():
            nc.vector.memset(carried[:, 1:2], 0.0)

        def carry_wait_pool(earlier):
            if not isinstance(earlier, int) or earlier > 0:
                nc.gpsimd.wait_ge(pool_carried, earlier)
            nc.gpsimd.tensor_tensor(carried[:, 0:1], minus_half[:, 0:1], minus_half[:, 0:1], ALU.mult
                                    ).then_inc(pool_carried, 1)

        block = stack.enter_context(nc.Block())

        @block.sync
        def _(sp):
            def load(t):
                if not t.exists():
                    return
                src = x_t[bass.ds(t.n, 1)].rearrange("a p n -> (a p) n")
                src_c = c_t[bass.ds(t.n, 1)].rearrange("a p n -> (a p) n")
                if t.at_least(2):
                    sp.wait_ge(x2_sb, t.n - 1)
                    sp.wait_ge(ctxT_ps, t.n - 1)
                sp.dma_start(x_sb[t.par][:], src).then_inc(x_in[t.par], 16)
                sp.dma_start(c_sb[t.par][:], src_c).then_inc(c_in[t.par], 16)

            def store(t):
                if not t.exists():
                    return
                sp.wait_ge(out_ready, t.n + 1)
                sp.dma_start(out_t[bass.ds(t.n, 1)].rearrange("a p n -> (a p) n"),
                             out_sb[t.par][:]).then_inc(stored[t.par], 16)

            sp.dma_start(x_sb[0][:], x_t[0]).then_inc(x_in[0], 16)
            sp.dma_start(cst[:], consts).then_inc(consts_in, 16)
            sp.dma_start(c_sb[0][:], c_t[0]).then_inc(c_in[0], 16)
            sp.dma_start(vec[:], vecs).then_inc(weights_in, 16)
            for dst, src in ((w_k, wk), (w_v, wv), (w_q, wq), (w_c, wc), (w_r, router), (w_s1, sw1)):
                sp.dma_start(dst[:], src).then_inc(weights_in, 16)
            sp.dma_start(w_s2[:], sw2.rearrange("(c p) o -> p c o", p=P)).then_inc(weights_in, 16)
            sp.dma_start(tab[:], tables).then_inc(weights_in, 16)
            sp.dma_start(x_sb[1][:], x_t[1]).then_inc(x_in[1], 16)
            sp.dma_start(c_sb[1][:], c_t[1]).then_inc(c_in[1], 16)
            sp.wait_ge(setup, 1)
            sp.dma_start(rows_dram[PAD_ROW:PAD_ROW + TILE].rearrange("(p s) n -> p (s n)", s=SUB),
                         pad[:]).then_inc(pads_in, 16)
            sp.dma_start(out[TOKENS:OUT_ROWS].rearrange("(p s) n -> p s n", s=SUB),
                         pad[:, :, 0:D]).then_inc(dummies_in, 16)

            def step(t):
                store(t.later(-1))
                if t.exists():
                    load(t.later(2))

            pipeline(sp, step)

            sp.wait_ge(table_done, 1)
            for e in range(E):
                at = sp.value_load(pad_at[0:1, e:e + 1], min_val=e * REGION, max_val=e * REGION + TOKENS)
                sp.dma_start(rows_dram[bass.ds(at, TILE)].rearrange("(p s) n -> p (s n)", s=SUB),
                             pad[:]).then_inc(pads_in, 16)
            sp.wait_ge(pads_in, 16 * (E + 1))
            for k in range(2):
                sp.wait_ge(scattered[k], SCAT_ALL)

            def expert_load(i, u):
                j = i * DEEP + u
                row = sp.value_load(row_of[0:1, bass.ds(j, 1)], min_val=0, max_val=PAD_ROW)
                e = sp.value_load(expert_of[0:1, bass.ds(j, 1)], min_val=0, max_val=E - 1)
                if not isinstance(i, int) or i > 0:
                    sp.wait_ge(added, 16 * SUB * (j - DEEP + 1))
                sp.dma_start(xb[u][:], rows_dram[bass.ds(row, TILE)].rearrange("(p s) n -> p (s n)", s=SUB)
                             ).then_inc(xb_in[u], 16)
                sp.dma_start(w1b[u][:], ew1[bass.ds(e, 1)].rearrange("a p n -> (a p) n")
                             ).then_inc(wb_in[u], 16)
                sp.dma_start(w2b[u][:], ew2[bass.ds(e, 1)].rearrange("a (c p) n -> p (a c) n", p=P)
                             ).then_inc(wb_in[u], 16)
                sp.dma_start(exb[u][:], extra[bass.ds(e, 1)].rearrange("a p n -> (a p) n")
                             ).then_inc(wb_in[u], 16)

            experts(sp, expert_load)
            sp.wait_ge(added, 16 * SUB * XTILES)

        @block.tensor
        def _(pe):
            mm, tr = nc.tensor.matmul, nc.tensor.transpose
            pe.wait_ge(consts_in, 16)
            pe.wait_ge(weights_in, 16 * 9)

            def turn(dst, src, width=D):
                for s in range(SUB):
                    last = tr(dst[:, s * P:(s + 1) * P], src(s), ident)
                return last

            def step(t):
                u, v = t.later(-1), t.later(-2)
                if t.exists():
                    pe.wait_ge(c_in[t.par], 16 * (t.half + 1))
                    if t.at_least(1):
                        pe.wait_ge(projT_sb, t.n)
                    turn(ps_ctxT, lambda s: c_sb[t.par][:, s, :]).then_inc(ctxT_ps, 1)
                    pe.wait_ge(xn_sb, t.n + 1)
                    if t.at_least(1):
                        pe.wait_ge(x2_sb, t.n)
                    turn(ps_xT, lambda s: xn[:, s, :]).then_inc(xT_ps, 1)
                    pe.wait_ge(ctxT_sb, t.n + 1)
                    mm(ps_k[:], w_k[:], ctxT[:], start=True, stop=True).then_inc(k_ps, 1)
                    mm(ps_v[:], w_v[:], ctxT[:], start=True, stop=True).then_inc(v_ps, 1)
                    pe.wait_ge(xnT_sb, t.n + 1)
                    mm(ps_q[:], w_q[:], xnT[:], start=True, stop=True).then_inc(q_ps, 1)
                if v.exists() and v.at_least(0):
                    pe.wait_ge(routed, v.n + 1)
                    mm(ps_rank, before, chosen[:].rearrange("p s e -> p (s e)"), start=True, stop=False)
                    mm(ps_rank, ones, seen[:, 0:SUB, :].rearrange("p s e -> p (s e)"), start=False,
                       stop=True).then_inc(rank_ps, 1)
                if u.exists() and u.at_least(0):
                    pe.wait_ge(rows_sb, u.n + 1)
                    if u.at_least(1):
                        pe.wait_ge(out_ready, u.n)
                    turn(ps_nT, lambda s: rows[u.par][:, s, 0:D]).then_inc(nT_ps, 1)
                if t.exists():
                    pe.wait_ge(kT_sb, t.n + 1)
                    mm(ps_csum[:], heads, kT[:], start=True, stop=True).then_inc(csum_ps, 1)
                if u.exists() and u.at_least(0):
                    pe.wait_ge(nT_sb, u.n + 1)
                    if u.at_least(1):
                        pe.wait_ge(place_sb, u.n)
                    for s in range(SUB):
                        last = mm(ps_logit[:, s * E:(s + 1) * E], nT[:, s * P:(s + 1) * P], w_r[:],
                                  start=True, stop=True)
                    last.then_inc(logit_ps, 1)
                    for c in range(HC):
                        mm(ps_h[c][:], w_s1[:, c * P:(c + 1) * P], nT[:], start=True, stop=True
                           ).then_inc(h_ps, 1)
                    if t.exists():
                        pe.wait_ge(q_parts, t.n + 1)
                    for c in range(HC):
                        pe.wait_ge(h_sb, u.n * HC + c + 1)
                        last = mm(ps_yT[:], w_s2[:, c, :], hT[:, c, :], start=(c == 0), stop=(c == HC - 1))
                    last.then_inc(yT_ps, 1)
                if t.exists():
                    pe.wait_ge(attn_sb, t.n + 1)
                    mm(ps_projT[:], w_c[:], attnT[:], start=True, stop=True).then_inc(projT_ps, 1)
                if u.exists() and u.at_least(0):
                    pe.wait_ge(yT_sb, u.n + 1)
                    turn(ps_y, lambda s: yT[:, s * P:(s + 1) * P]).then_inc(y_ps, 1)
                if t.exists():
                    pe.wait_ge(projT_sb, t.n + 1)
                    turn(ps_proj, lambda s: projT[:, s * P:(s + 1) * P]).then_inc(proj_ps, 1)

            pipeline(pe, step)
            pe.wait_ge(place_sb, TILES)
            mm(ps_count, ones, seen[:, SUB, :], start=True, stop=True).then_inc(count_ps, 1)

            def turn_in(i, u):
                j = i * DEEP + u
                pe.wait_ge(xb_in[u], 16 * (i + 1))
                turn(pb_xT, lambda s: xb[u][:, s, 0:D]).then_inc(bxT_ps, 1)

            def turn_out(i, u):
                j = i * DEEP + u
                pe.wait_ge(byT_sb, j + 1)
                if not isinstance(i, int) or j > 0:
                    pe.wait_ge(by_sb, j)
                turn(pb_y, lambda s: yT[:, s * P:(s + 1) * P]).then_inc(by_ps, 1)

            def expert_step(i, u):
                j = i * DEEP + u
                first = isinstance(i, int) and j == 0
                last_tile = isinstance(i, int) and j == XTILES - 1
                if first:
                    pe.wait_ge(out_ready, TILES)
                    turn_in(i, u)
                pe.wait_ge(bxT_sb, j + 1)
                pe.wait_ge(wb_in[u], 16 * 3 * (i + 1))
                for c in range(HC):
                    mm(pb_h[c][:], w1b[u][:, c * P:(c + 1) * P], xnT[:], start=True, stop=True
                       ).then_inc(bh_ps, 1)
                if not first:
                    turn_out(i - (u == 0), (u - 1) % DEEP)
                if not last_tile:
                    turn_in(i + (u == DEEP - 1), (u + 1) % DEEP)
                for c in range(HC):
                    pe.wait_ge(bh_sb, j * HC + c + 1)
                    last = mm(pb_yT[:], w2b[u][:, c, :], hT[:, c, :], start=(c == 0), stop=(c == HC - 1))
                last.then_inc(byT_ps, 1)
                if last_tile:
                    turn_out(i, u)

            experts(pe, expert_step)

        @block.scalar
        def _(act):
            fn = nc.scalar.activation

            def feature(col):
                return vec[:, col:col + 1]

            def normalise(which, dst, src):
                for s in range(SUB):
                    last = fn(dst(s), src(s), ACT.Identity, bias=shift[which][:, s:s + 1],
                              scale=rstd[which][:, s:s + 1])
                return last

            def norm_x(t):
                if t.exists():
                    act.wait_ge(shift_sb[0], t.n + 1)
                    normalise(0, lambda s: xn[:, s, :], lambda s: x_sb[t.par][:, s, :]).then_inc(xn_sb, 1)

            act.wait_ge(weights_in, 16 * 9)
            norm_x(FIRST)

            def step(t):
                u = t.later(-1)
                has_u = u.exists() and u.at_least(0)
                if t.exists():
                    act.wait_ge(ctxT_ps, t.n + 1)
                    fn(ctxT[:], ps_ctxT[:], ACT.Copy).then_inc(ctxT_sb, 1)
                    act.wait_ge(k_ps, t.n + 1)
                    fn(k_exp[:], ps_k[:], ACT.Exp, bias=feature(V_BK))
                    fn(k_lin[:], ps_k[:], ACT.Relu, bias=feature(V_BK)).then_inc(k_parts, 1)
                if has_u:
                    act.wait_ge(shift_sb[1], u.n + 1)
                    if u.at_least(2):
                        act.wait_ge(scattered[u.par], 16 * SCATTERS * u.half)
                    normalise(1, lambda s: rows[u.par][:, s, 0:D], lambda s: x2[:, s, :]).then_inc(rows_sb, 1)
                if t.exists():
                    act.wait_ge(q_ps, t.n + 1)
                    fn(q_exp[:], ps_q[:], ACT.Exp, bias=feature(V_BQ))
                    fn(q_lin[:], ps_q[:], ACT.Relu, bias=feature(V_BQ)).then_inc(q_parts, 1)
                if has_u:
                    for c in range(HC):
                        act.wait_ge(h_ps, u.n * HC + c + 1)
                        fn(hT[:, c, :], ps_h[c][:], ACT.Relu, bias=feature(V_SB1 + c)).then_inc(h_sb, 1)
                        if c == 0:
                            act.wait_ge(key_sb, u.n + 1)
                            fn(e_neg[:], key[:], ACT.Exp, scale=-1.0).then_inc(e_sb, 1)
                norm_x(t.later(1))
                if has_u:
                    act.wait_ge(yT_ps, u.n + 1)
                    fn(yT[:], ps_yT[:], ACT.Identity, bias=feature(V_SB2)).then_inc(yT_sb, 1)
                if t.exists():
                    act.wait_ge(projT_ps, t.n + 1)
                    fn(projT[:], ps_projT[:], ACT.Identity, bias=feature(V_BC)).then_inc(projT_sb, 1)

            pipeline(act, step)

            def expert_step(i, u):
                j = i * DEEP + u
                act.wait_ge(wb_in[u], 16 * 3 * (i + 1))
                for c in range(HC):
                    act.wait_ge(bh_ps, j * HC + c + 1)
                    fn(hT[:, c, :], pb_h[c][:], ACT.Relu, bias=exb[u][:, COL_B1 + c:COL_B1 + c + 1]
                       ).then_inc(bh_sb, 1)

            experts(act, expert_step)

        @block.gpsimd
        def _(pool):
            def scatter(t, which):
                for s in range(SUB):
                    pool.indirect_dma_start(
                        rows_dram, bass.IndirectOffsetOnAxis(ap=slot[t.par][:, which, s:s + 1], axis=0),
                        rows[t.par][:, s, :], None).then_inc(scattered[t.par], 16)

            def raise_power(which, t):
                pool.wait_ge(spread_sb[which], t.n + 1)
                nc.gpsimd.tensor_tensor(rstd[which][:], spread[which][:], minus_half[:], ALU.pow
                                        ).then_inc(power[which], 1)
                pool.wait_ge(power[which], t.n + 1)
                nc.gpsimd.tensor_tensor(shift[which][:], neg_mean[which][:], rstd[which][:], ALU.mult
                                        ).then_inc(shift_sb[which], 1)

            pool.wait_ge(setup, 1)
            raise_power(0, FIRST)

            def step(t):
                v = t.later(-2)
                has_v = v.exists() and v.at_least(0)
                if has_v:
                    pool.wait_ge(slot_sb, v.n + 1)
                    pool.wait_ge(routed, v.n + 1)
                    pool.wait_ge(rows_sb, v.n + 1)
                    carry_wait_pool(v.n)
                    scatter(v, 0)
                if t.later(1).exists():
                    raise_power(0, t.later(1))
                if has_v:
                    scatter(v, 1)
                if t.exists():
                    raise_power(1, t)

            pipeline(pool, step)
            for k in range(2):
                pool.wait_ge(stored[k], 16 * TILES // 2)
            pool.wait_ge(dummies_in, 16)

            def expert_step(i, u):
                j = i * DEEP + u
                pool.wait_ge(by_sb, j + 1)
                if not isinstance(i, int) or j > 0:
                    pool.wait_ge(added, 16 * SUB * j)
                carry_wait_pool(TILES + j)
                for s in range(SUB):
                    pool.indirect_dma_start(
                        out, bass.IndirectOffsetOnAxis(ap=tok[u][:, s:s + 1], axis=0),
                        yb[u][:, s, :], None, compute_op=ALU.add).then_inc(added, 16)

            experts(pool, expert_step)

        @block.vector
        def _(dve):
            v_ = nc.vector

            def feature(col):
                return vec[:, col:col + 1]

            class Steps:

                def __init__(self, sem, n, per):
                    self.sem, self.start, self.k = sem, n * per, 0

                def then(self, ins):
                    ins.then_inc(self.sem, 1)
                    self.k += 1

                def wait(self):
                    dve.wait_ge(self.sem, self.start + self.k)

            STAT_STEPS = 2

            def statistics(which, t, src):
                c = Steps(stat[which], t.n, STAT_STEPS)
                for s in range(SUB):
                    last = v_.bn_stats(st[which][:, s, :], src[:, s, :])
                c.then(last)
                c.wait()
                carry_wait_dve()
                for s in range(SUB):
                    last = v_.bn_aggr(mv[which][:, s, :], st[which][:, s, :])
                c.then(last)
                c.wait()
                if t.at_least(1):
                    dve.wait_ge(shift_sb[which], t.n)
                v_.tensor_scalar(neg_mean[which][:], mv[which][:, :, 0], -1.0, None, ALU.mult)
                if which == 0:
                    scale, eps = 1.0, LN_EPS
                else:
                    scale, eps = 1.0 + RMS_EPS, LN_EPS * RMS_EPS
                v_.tensor_scalar(spread[which][:], mv[which][:, :, 1], scale, eps, ALU.mult, ALU.add
                                 ).then_inc(spread_sb[which], 1)

            def stats_x(t):
                if t.exists():
                    dve.wait_ge(x_in[t.par], 16 * (t.half + 1))
                    statistics(0, t, x_sb[t.par])

            dve.wait_ge(consts_in, 16)
            v_.memset(minus_half[:], -0.5)
            v_.memset(seen[:], 0.0)
            v_.memset(pad[:, :, 0:COL_ID], 0.0)
            v_.memset(pad[:, :, COL_ID + 1:ROW], 0.0)
            for k in range(2):
                v_.memset(rows[k][:, :, COL_ID + 1:ROW], 0.0)
            v_.tensor_scalar(rows[1][:, :, COL_ID], id0, float(-TILE), None, ALU.add)
            v_.tensor_scalar(pad[:, :, COL_ID], id0, float(TOKENS), None, ALU.add).then_inc(setup, 1)
            dve.wait_ge(setup, 1)
            stats_x(FIRST)
            dve.wait_ge(weights_in, 16 * 9)

            def over_experts(ap):
                return ap.unsqueeze(2).to_broadcast([P, SUB, E])

            ROUTE_STEPS = 22

            def route_tile(u):
                c = Steps(route, u.n, ROUTE_STEPS)

                def do(ins):
                    c.then(ins)
                    c.wait()

                for which, keys in ((0, key), (1, key2)):
                    do(v_.tensor_reduce(best[:], keys[:], AX, ALU.max))
                    do(v_.tensor_tensor(hit[:], keys[:], over_experts(best[:]), ALU.is_equal))
                    do(v_.tensor_tensor(ranked[:], hit[:], order, ALU.mult))
                    do(v_.tensor_reduce(best[:], ranked[:], AX, ALU.max))
                    do(v_.tensor_tensor(hot[:, which], ranked[:], over_experts(best[:]), ALU.is_equal))
                    if which == 0:
                        do(v_.scalar_tensor_tensor(key2[:], hot[:, 0], -1e30, key[:], ALU.mult, ALU.add))
                do(v_.tensor_tensor(chosen[:], hot[:, 0], hot[:, 1], ALU.add))
                do(v_.tensor_copy(seen[:, 0, :], seen[:, SUB, :]))
                for s in range(SUB):
                    do(v_.tensor_tensor(seen[:, s + 1, :], seen[:, s, :], chosen[:, s, :], ALU.add))
                dve.wait_ge(e_sb, u.n + 1)
                do(v_.tensor_scalar(den[:], e_neg[:], 1.0, None, ALU.add))
                do(v_.reciprocal(prob[:], den[:]))
                do(v_.tensor_tensor(score[:], prob[:], chosen[:], ALU.mult))
                do(v_.tensor_reduce(total[:], score[:], AX, ALU.add))
                do(v_.tensor_scalar(inv_total[:], total[:], COMB_EPS, None, ALU.add))
                assert c.k == ROUTE_STEPS, c.k
                v_.reciprocal(total[:], inv_total[:]).then_inc(inv_total_sb, 1)
                dve.wait_ge(inv_total_sb, u.n + 1)
                if u.at_least(2):
                    dve.wait_ge(scattered[u.par], 16 * SCATTERS * u.half)
                v_.tensor_tensor(rows[u.par][:, :, COL_W:COL_W + E], score[:], over_experts(total[:]), ALU.mult)
                v_.tensor_scalar(rows[u.par][:, :, COL_ID], rows[1 - u.par][:, :, COL_ID], float(TILE), None,
                                 ALU.add).then_inc(routed, 1)

            def step(t):
                u, v = t.later(-1), t.later(-2)
                has_u, has_v = u.exists() and u.at_least(0), v.exists() and v.at_least(0)
                if t.exists():
                    dve.wait_ge(xT_ps, t.n + 1)
                    v_.tensor_copy(xnT[:], ps_xT[:]).then_inc(xnT_sb, 1)
                    dve.wait_ge(k_parts, t.n + 1)
                    v_.scalar_tensor_tensor(kT[:], k_exp[:], 1.0, k_lin[:], ALU.min, ALU.add
                                            ).then_inc(kT_sb, 1)
                if has_v:
                    dve.wait_ge(rank_ps, v.n + 1)
                    dve.wait_ge(routed, v.n + 1)
                    v_.tensor_tensor(place[:], ps_rank.rearrange("p (s e) -> p s e", s=SUB), base, ALU.add
                                     ).then_inc(place_sb, 1)
                    dve.wait_ge(place_sb, v.n + 1)
                    for i in range(TOPK):
                        last = v_.tensor_tensor(placed[:, i], hot[:, i], place[:], ALU.mult)
                    last.then_inc(placed_sb, 1)
                    dve.wait_ge(placed_sb, v.n + 1)
                    if v.at_least(2):
                        dve.wait_ge(scattered[v.par], 16 * SCATTERS * v.half)
                    v_.tensor_reduce(slot_f[:], placed[:], AX, ALU.add).then_inc(slot_f_sb, 1)
                    dve.wait_ge(slot_f_sb, v.n + 1)
                    v_.tensor_copy(slot[v.par][:], slot_f[:]).then_inc(slot_sb, 1)
                if has_u:
                    dve.wait_ge(nT_ps, u.n + 1)
                    v_.tensor_scalar(nT[:], ps_nT[:], feature(V_NW), None, ALU.mult).then_inc(nT_sb, 1)
                if t.exists():
                    dve.wait_ge(q_parts, t.n + 1)
                    v_.scalar_tensor_tensor(qT[:], q_exp[:], 1.0, q_lin[:], ALU.min, ALU.add
                                            ).then_inc(qT_sb, 1)
                if has_u:
                    dve.wait_ge(logit_ps, u.n + 1)
                    v_.tensor_scalar(key[:], ps_logit.rearrange("p (s e) -> p s e", s=SUB), SIG_ONE, SIG_ZERO,
                                     ALU.min, ALU.max).then_inc(key_sb, 1)
                stats_x(t.later(1))
                if t.exists():
                    dve.wait_ge(csum_ps, t.n + 1)
                    v_.reciprocal(k_inv[:], ps_csum[:]).then_inc(inv_sb, 1)
                    dve.wait_ge(qT_sb, t.n + 1)
                    v_.tensor_tensor(qk[:], qT[:], kT[:], ALU.mult).then_inc(qk_sb, 1)
                    dve.wait_ge(inv_sb, t.n + 1)
                    dve.wait_ge(qk_sb, t.n + 1)
                    v_.tensor_tensor(qkn[:], qk[:], k_inv[:], ALU.mult).then_inc(qkn_sb, 1)
                    dve.wait_ge(qkn_sb, t.n + 1)
                    dve.wait_ge(v_ps, t.n + 1)
                    v_.scalar_tensor_tensor(attnT[:], ps_v[:], feature(V_BV), qkn[:], ALU.add, ALU.mult
                                            ).then_inc(attn_sb, 1)
                if has_u:
                    dve.wait_ge(key_sb, u.n + 1)
                    route_tile(u)
                    dve.wait_ge(y_ps, u.n + 1)
                    if u.at_least(2):
                        dve.wait_ge(stored[u.par], 16 * u.half)
                    v_.tensor_tensor(out_sb[u.par][:].rearrange("p s d -> p (s d)"), ps_y[:],
                                     x2[:].rearrange("p s d -> p (s d)"), ALU.add).then_inc(out_ready, 1)
                if t.exists():
                    dve.wait_ge(proj_ps, t.n + 1)
                    if has_u:
                        dve.wait_ge(out_ready, u.n + 1)
                    v_.tensor_tensor(x2[:].rearrange("p s d -> p (s d)"), ps_proj[:],
                                     x_sb[t.par][:].rearrange("p s d -> p (s d)"), ALU.add).then_inc(x2_sb, 1)
                    dve.wait_ge(x2_sb, t.n + 1)
                    statistics(1, t, x2)

            pipeline(dve, step)

            c = Steps(table, 0, 0)

            def do(ins):
                c.then(ins)
                c.wait()

            step_t = tab[:, TB_STEP:TB_UPTO].rearrange("a (e m) -> a e m", e=E)
            upto_t = tab[:, TB_UPTO:TB_TILE].rearrange("a (e m) -> a e m", e=E)
            tile_t, reg_t = tab[:, TB_TILE:TB_REG], tab[:, TB_REG:TB_REG + E]
            dve.wait_ge(count_ps, 1)
            do(v_.tensor_copy(cnt[:], ps_count[0:1, :]))
            v_.tensor_tensor(pad_at[:], cnt[:], reg_t, ALU.add)
            do(v_.tensor_tensor(tl_a[:], cnt[:].unsqueeze(2).to_broadcast([1, E, TILES]), step_t, ALU.is_gt))
            do(v_.tensor_reduce(tl_n[:], tl_a[:], AX, ALU.add))
            do(v_.tensor_tensor(tl_b[:], tl_n[:].unsqueeze(1).to_broadcast([1, E, E]), upto_t, ALU.mult))
            do(v_.tensor_reduce(tl_end[:], tl_b[:], AX, ALU.add))
            many = [1, XTILES, E]
            do(v_.tensor_tensor(tl_past[:], tile_t.unsqueeze(2).to_broadcast(many),
                                tl_end[:].unsqueeze(1).to_broadcast(many), ALU.is_ge))
            do(v_.tensor_reduce(tl_e[:], tl_past[:], AX, ALU.add))
            do(v_.tensor_tensor(tl_used[:], tl_past[:], tl_n[:].unsqueeze(1).to_broadcast(many), ALU.mult))
            do(v_.tensor_reduce(tl_first[:], tl_used[:], AX, ALU.add))
            do(v_.tensor_tensor(tl_k[:], tile_t, tl_first[:], ALU.subtract))
            do(v_.tensor_scalar(tl_base[:], tl_e[:], float(REGION), None, ALU.mult))
            do(v_.scalar_tensor_tensor(tl_row[:], tl_k[:], float(TILE), tl_base[:], ALU.mult, ALU.add))
            do(v_.tensor_scalar(expert_of[:], tl_e[:], float(E - 1), None, ALU.min))
            v_.tensor_scalar(row_of[:], tl_row[:], float(PAD_ROW), None, ALU.min).then_inc(table_done, 1)

            def finish(i, u):
                j = i * DEEP + u
                dve.wait_ge(by_ps, j + 1)
                dve.wait_ge(w_sb, j + 1)
                for s in range(SUB):
                    last = v_.tensor_scalar(yb[u][:, s, :], pb_y[:, s * P:(s + 1) * P], w_row[:, s:s + 1], None,
                                            ALU.mult)
                last.then_inc(by_sb, 1)

            def turned(i, u):
                j = i * DEEP + u
                dve.wait_ge(bxT_ps, j + 1)
                v_.tensor_scalar(xnT[:], pb_xT[:], feature(V_NW), None, ALU.mult).then_inc(bxT_sb, 1)

            def expert_step(i, u):
                j = i * DEEP + u
                first = isinstance(i, int) and j == 0
                last_tile = isinstance(i, int) and j == XTILES - 1
                if first:
                    turned(i, u)
                else:
                    finish(i - (u == 0), (u - 1) % DEEP)
                if not last_tile:
                    turned(i + (u == DEEP - 1), (u + 1) % DEEP)
                dve.wait_ge(xb_in[u], 16 * (i + 1))
                dve.wait_ge(wb_in[u], 16 * 3 * (i + 1))
                v_.tensor_tensor(w_pick[:], xb[u][:, :, COL_W:COL_W + E],
                                 exb[u][:, COL_HOT:COL_HOT + E].unsqueeze(1).to_broadcast([P, SUB, E]), ALU.mult
                                 ).then_inc(pick_sb, 1)
                v_.tensor_copy(tok[u][:], xb[u][:, :, COL_ID])
                dve.wait_ge(pick_sb, j + 1)
                if not first:
                    dve.wait_ge(by_sb, j)
                v_.tensor_reduce(w_row[:], w_pick[:], AX, ALU.add).then_inc(w_sb, 1)
                dve.wait_ge(byT_ps, j + 1)
                v_.tensor_scalar(yT[:], pb_yT[:], exb[u][:, COL_B2:COL_B2 + 1], None, ALU.add
                                 ).then_inc(byT_sb, 1)
                if last_tile:
                    finish(i, u)

            experts(dve, expert_step)


def kernel(**inputs):
    import concourse.bacc as bacc
    from concourse.bass_utils import run_bass_kernel_spmd

    def given(name):
        return np.asarray(inputs[name])

    ffn, att = "L0_ffn_", "L0_xattn_"
    consts, tables = constants()
    columns = [given(att + n)[:, None] for n in ("wq_b", "wk_b", "wv_b", "wc_b")]
    columns += [given(ffn + "norm_weight")[:, None], given(ffn + "sb1").reshape(HC, P).T, given(ffn + "sb2")[:, None]]
    hot = np.broadcast_to(np.eye(E, dtype=np.float32)[:, None, :], (E, P, E))
    extra = np.concatenate([given(ffn + "eb1").reshape(E, HC, P).transpose(0, 2, 1),
                            given(ffn + "eb2")[:, :, None], hot], axis=2)
    arrays = {
        "x": given("x").reshape(TOKENS, D),
        "ctx_in": given("ctx_1024").reshape(TOKENS, D),
        "wq": given(att + "wq_w"), "wk": given(att + "wk_w"), "wv": given(att + "wv_w"), "wc": given(att + "wc_w"),
        "vecs": np.concatenate(columns, axis=1),
        "router": given(ffn + "router_w").T,
        "sw1": given(ffn + "sw1"), "sw2": given(ffn + "sw2"),
        "ew1": given(ffn + "ew1"), "ew2": given(ffn + "ew2"),
        "extra": extra, "consts": consts, "tables": tables,
    }
    arrays = {name: np.ascontiguousarray(a) for name, a in arrays.items()}
    nc = bacc.Bacc("TRN2", target_bir_lowering=False, num_devices=1)
    aps = {name: nc.dram_tensor(name, a.shape, mybir.dt.from_np(a.dtype), kind="ExternalInput").ap()
           for name, a in arrays.items()}
    rows_dram = nc.dram_tensor("rows_dram", (X_ROWS, ROW), F32, kind="Internal").ap()
    out = nc.dram_tensor("out", (OUT_ROWS, D), F32, kind="ExternalOutput").ap()
    token_kernel(nc, **aps, rows_dram=rows_dram, out=out)
    result = run_bass_kernel_spmd(nc, [arrays], core_ids=[0]).results[0]["out"]
    return result[:TOKENS].reshape(128, 64, D)
```

```python
from contextlib import ExitStack

import numpy as np

import concourse.bass as bass
from concourse import mybir

F32 = mybir.dt.float32
BF16 = mybir.dt.bfloat16
I32 = mybir.dt.int32
U32 = mybir.dt.uint32
ALU = mybir.AluOpType
ACT = mybir.ActivationFunctionType
AX = mybir.AxisListType.X

P = 128
D = 128
HID = 512
HC = HID // P
E = 8
TOPK = 2
HEADS, DEPTH = 16, 8
TOKENS = 128 * 64
SUB = 4
TILE = P * SUB
TILES = TOKENS // TILE
LN_EPS = 1e-5
RMS_EPS = 1e-8
COMB_EPS = 1e-6
SIG_ONE, SIG_ZERO = 16.635532, -88.0

COL_W, COL_ID, ROW = D, D + E, 140
REGION = TOKENS + TILE
PAD_ROW = E * REGION
X_ROWS = PAD_ROW + TILE
XTILES = TOPK * TOKENS // TILE + E - 1
OUT_ROWS = TOKENS + TILE
COL_B1, COL_B2, COL_HOT, EXTRA = 0, HC, HC + 1, HC + 1 + E
CM_IDENT, CM_BEFORE, CM_ONES, CM_HEADS = 0, P, 2 * P, 3 * P
CS_BASE, CS_EXPERT, CS_ID = 4 * P, 4 * P + SUB * E, 4 * P + SUB * E + E
CONSTS = CS_ID + SUB
TB_STEP, TB_UPTO, TB_TILE, TB_REG = 0, E * TILES, E * TILES + E * E, E * TILES + E * E + XTILES
TABLES = TB_REG + E
V_BQ, V_BK, V_BV, V_BC, V_NW, V_SB1, V_SB2 = 0, 1, 2, 3, 4, 5, 5 + HC
VECS = V_SB2 + 1


def constants():
    c = np.zeros((P, CONSTS), np.float32)
    i = np.arange(P)
    c[:, CM_IDENT:CM_IDENT + P] = np.eye(P)
    c[:, CM_BEFORE:CM_BEFORE + P] = i[:, None] < i[None, :]
    c[:, CM_ONES:CM_ONES + P] = 1
    same_place = i[:, None] % DEPTH == i[None, :] % DEPTH
    c[:, CM_HEADS:CM_HEADS + P] = same_place & (i[:, None] // DEPTH <= i[None, :] // DEPTH)
    c[:, CS_BASE:CS_BASE + SUB * E] = np.tile(np.arange(E) * REGION, SUB)
    c[:, CS_EXPERT:CS_EXPERT + E] = np.arange(E)
    c[:, CS_ID:CS_ID + SUB] = np.arange(TILE).reshape(P, SUB)
    t = np.zeros((1, TABLES), np.float32)
    t[0, TB_STEP:TB_UPTO] = np.tile(np.arange(TILES) * TILE, E)
    t[0, TB_UPTO:TB_TILE] = (np.arange(E)[None, :] <= np.arange(E)[:, None]).ravel()
    t[0, TB_TILE:TB_REG] = np.arange(XTILES)
    t[0, TB_REG:] = np.arange(E) * REGION
    return c, t


class Tile:

    def __init__(self, pair, offset):
        self.par = offset % 2
        self.half = pair + offset // 2
        self.n = 2 * pair + offset if isinstance(pair, int) else pair * 2 + offset
        self.static = isinstance(pair, int)
        self.pair, self.offset = pair, offset

    def later(self, k):
        return Tile(self.pair, self.offset + k)

    def at_least(self, k):
        return not self.static or self.n >= k

    def exists(self):
        return not self.static or 0 <= self.n < TILES


def token_kernel(nc, x, ctx_in, wq, wk, wv, wc, vecs, router, sw1, sw2, ew1, ew2, extra, consts, tables,
                 rows_dram, out):
    with ExitStack() as stack:
        def sb(name, shape, dt=F32):
            return stack.enter_context(nc.sbuf_tensor("sb_" + name, shape, dt))

        def bank(name):
            return stack.enter_context(nc.psum_tensor("ps_" + name, [P, TILE], F32))

        def sem(name):
            return stack.enter_context(nc.semaphore(name))

        def pair_of(make, name):
            return [make(f"{name}{k}") for k in range(2)]

        cst = sb("cst", [P, CONSTS])
        tab = sb("tab", [1, TABLES])
        vec = sb("vec", [P, VECS])
        w_q, w_k, w_v, w_c = (sb(n, [P, D]) for n in ("w_q", "w_k", "w_v", "w_c"))
        w_r = sb("w_r", [P, E])
        w_s1 = sb("w_s1", [P, HID])
        w_s2 = sb("w_s2", [P, HC, D])
        x_sb = [sb(f"x{k}", [P, SUB, D]) for k in range(2)]
        c_sb = [sb(f"c{k}", [P, SUB, D]) for k in range(2)]
        xn = sb("xn", [P, SUB, D])
        xnT, ctxT = sb("xnT", [P, TILE]), sb("ctxT", [P, TILE])
        k_exp, k_lin, q_exp, q_lin = (sb(n, [P, TILE]) for n in ("k_exp", "k_lin", "q_exp", "q_lin"))
        kT, qT = sb("kT", [P, TILE]), sb("qT", [P, TILE])
        k_inv, qk, qkn, attnT = (sb(n, [P, TILE]) for n in ("k_inv", "qk", "qkn", "attnT"))
        projT = sb("projT", [P, TILE])
        x2 = [sb(f"x2_{k}", [P, SUB, D]) for k in range(2)]
        rows = [sb(f"rows{k}", [P, SUB, ROW]) for k in range(2)]
        nT = [sb(f"nT{k}", [P, TILE]) for k in range(2)]
        hT = sb("hT", [P, HC, TILE])
        yT = sb("yT", [P, TILE])
        out_sb = [sb(f"out{k}", [P, SUB, D]) for k in range(2)]
        pad = sb("pad", [P, SUB, ROW])
        st = [sb(f"st{k}", [P, SUB, 6]) for k in range(2)]
        mv = [sb(f"mv{k}", [P, SUB, 2]) for k in range(2)]
        spread = [sb(f"spread{k}", [P, SUB]) for k in range(2)]
        neg_mean = [sb(f"neg_mean{k}", [P, SUB]) for k in range(2)]
        rstd = [sb(f"rstd{k}", [P, SUB]) for k in range(2)]
        shift = [sb(f"shift{k}", [P, SUB]) for k in range(2)]
        carried = sb("carried", [P, 2])
        minus_half = sb("minus_half", [P, SUB])
        key, e_neg, den, prob = (sb(n, [P, SUB, E]) for n in ("key", "e_neg", "den", "prob"))
        sorted_key, sorted_at = sb("sorted_key", [P, SUB, E]), sb("sorted_at", [P, SUB, E], U32)
        top_at = sb("top_at", [P, SUB, TOPK])
        hot = sb("hot", [P, TOPK, SUB, E])
        chosen = sb("chosen", [P, SUB, E], BF16)
        tile_count, seen = sb("tile_count", [P, E]), sb("seen", [P, E], BF16)
        before_b, ones_b = sb("before_b", [P, P], BF16), sb("ones_b", [P, P], BF16)
        score = sb("score", [P, SUB, E + 1])
        total, inv_total = sb("total", [P, SUB]), sb("inv_total", [P, SUB])
        place = sb("place", [P, SUB, E])
        placed = sb("placed", [P, TOPK, SUB, E])
        slot_f = sb("slot_f", [P, TOPK, SUB])
        slot = [sb(f"slot{k}", [P, TOPK, SUB], I32) for k in range(2)]
        cnt = sb("cnt", [1, E])
        tl_a, tl_n = sb("tl_a", [1, E, TILES]), sb("tl_n", [1, E])
        tl_b, tl_end = sb("tl_b", [1, E, E]), sb("tl_end", [1, E])
        tl_past, tl_used = sb("tl_past", [1, XTILES, E]), sb("tl_used", [1, XTILES, E])
        tl_e, tl_first = sb("tl_e", [1, XTILES]), sb("tl_first", [1, XTILES])
        tl_k, tl_base, tl_row = (sb(n, [1, XTILES]) for n in ("tl_k", "tl_base", "tl_row"))
        row_of, expert_of = sb("row_of", [1, XTILES], I32), sb("expert_of", [1, XTILES], I32)
        pad_at = sb("pad_at", [1, E], I32)
        DEEP = 3
        xb = [sb(f"xb{k}", [P, SUB, ROW]) for k in range(DEEP)]
        w1b = [sb(f"w1b{k}", [P, HID]) for k in range(DEEP)]
        w2b = [sb(f"w2b{k}", [P, HC, D]) for k in range(DEEP)]
        exb = [sb(f"exb{k}", [P, EXTRA]) for k in range(DEEP)]
        yb = [sb(f"yb{k}", [P, SUB, D]) for k in range(DEEP)]
        tok = [sb(f"tok{k}", [P, SUB], I32) for k in range(DEEP)]
        w_pick, w_row = sb("w_pick", [P, SUB, E]), sb("w_row", [P, SUB])

        b = [bank(f"b{k}") for k in range(8)]
        ps_ctxT, ps_xT, ps_k, ps_v, ps_q, ps_csum = b[0], b[1], b[2], b[3], b[4], b[6]
        ps_projT, ps_proj, ps_nT, ps_yT, ps_y = b[0], b[1], b[5], b[4], b[5]
        ps_h = [b[5], b[0], b[1], b[2]]
        ps_logit, ps_rank, ps_count = b[7][:, 0:SUB * E], b[7][:, 64:64 + SUB * E], b[6][:, 0:E]
        pb_xT, pb_h, pb_yT, pb_y = b[0], b[1:5], b[5], b[6]

        ident, heads = cst[:, CM_IDENT:CM_IDENT + P], cst[:, CM_HEADS:CM_HEADS + P]
        base = cst[:, CS_BASE:CS_BASE + SUB * E].rearrange("p (s e) -> p s e", s=SUB)
        expert_no = cst[:, CS_EXPERT:CS_EXPERT + E]
        id0 = cst[:, CS_ID:CS_ID + SUB]

        consts_in = sem("consts_in")
        weights_in = sem("weights_in")
        x_in, c_in = pair_of(sem, "x_in"), pair_of(sem, "c_in")
        setup = sem("setup")
        ctxT_ps, xT_ps, k_ps, v_ps, q_ps = (sem(n) for n in ("ctxT_ps", "xT_ps", "k_ps", "v_ps", "q_ps"))
        csum_ps, projT_ps, proj_ps = sem("csum_ps"), sem("projT_ps"), sem("proj_ps")
        rank_ps, nT_ps, logit_ps = sem("rank_ps"), sem("nT_ps"), sem("logit_ps")
        h_ps, yT_ps, y_ps, count_ps = sem("h_ps"), sem("yT_ps"), sem("y_ps"), sem("count_ps")
        ctxT_sb, k_parts, q_parts = sem("ctxT_sb"), sem("k_parts"), sem("q_parts")
        xn_sb, rows_sb, e_sb = sem("xn_sb"), sem("rows_sb"), sem("e_sb")
        h_sb, yT_sb, projT_sb = sem("h_sb"), sem("yT_sb"), sem("projT_sb")
        xnT_sb, kT_sb, qT_sb, nT_sb = sem("xnT_sb"), sem("kT_sb"), sem("qT_sb"), sem("nT_sb")
        inv_sb, qk_sb, qkn_sb, attn_sb = sem("inv_sb"), sem("qk_sb"), sem("qkn_sb"), sem("attn_sb")
        place_sb, placed_sb, slot_f_sb, slot_sb = (sem(n) for n in ("place_sb", "placed_sb", "slot_f_sb", "slot_sb"))
        key_sb, routed, out_ready, x2_sb = sem("key_sb"), sem("routed"), sem("out_ready"), sem("x2_sb")
        counted, seen_sb = sem("counted"), sem("seen_sb")
        route = sem("route")
        stat = [sem("stat1"), sem("stat2")]
        spread_sb = [sem("spread1"), sem("spread2")]
        power = [sem("power1"), sem("power2")]
        shift_sb = [sem("shift1"), sem("shift2")]
        stored = pair_of(sem, "stored")
        scattered = pair_of(sem, "scattered")
        SCATTERS = TOPK * SUB
        table = sem("table")
        table_done = sem("table_done")
        pads_in = sem("pads_in")
        dummies_in = sem("dummies_in")
        pool_carried = sem("pool_carried")
        xb_in = [sem(f"xb_in{k}") for k in range(DEEP)]
        wb_in = [sem(f"wb_in{k}") for k in range(DEEP)]
        bxT_ps, bh_ps, byT_ps, by_ps = sem("bxT_ps"), sem("bh_ps"), sem("byT_ps"), sem("by_ps")
        bxT_sb, bh_sb, byT_sb, by_sb = sem("bxT_sb"), sem("bh_sb"), sem("byT_sb"), sem("by_sb")
        pick_sb, w_sb = sem("pick_sb"), sem("w_sb")
        added = sem("added")

        x_t = x.rearrange("(t p s) d -> t p (s d)", p=P, s=SUB)
        c_t = ctx_in.rearrange("(t p s) d -> t p (s d)", p=P, s=SUB)
        out_t = out.rearrange("(t p s) d -> t p (s d)", p=P, s=SUB)
        FIRST = Tile(0, 0)
        SCAT_ALL = 16 * SCATTERS * TILES // 2

        def pipeline(engine, step):
            for t in range(4):
                step(Tile(0, t))
            with engine.Fori(2, TILES // 2 - 1) as pair:
                step(Tile(pair, 0))
                step(Tile(pair, 1))
            for t in range(TILES - 2, TILES + 2):
                step(Tile(0, t))

        def experts(engine, step):
            for u in range(DEEP):
                step(0, u)
            with engine.Fori(1, XTILES // DEEP - 1) as i:
                for u in range(DEEP):
                    step(i, u)
            for u in range(DEEP):
                step(XTILES // DEEP - 1, u)

        assert XTILES % DEEP == 0

        def carry_wait_dve():
            nc.vector.memset(carried[:, 1:2], 0.0)

        def carry_wait_pool(earlier):
            if not isinstance(earlier, int) or earlier > 0:
                nc.gpsimd.wait_ge(pool_carried, earlier)
            nc.gpsimd.tensor_tensor(carried[:, 0:1], minus_half[:, 0:1], minus_half[:, 0:1], ALU.mult
                                    ).then_inc(pool_carried, 1)

        block = stack.enter_context(nc.Block())

        @block.sync
        def _(sp):
            def load(t):
                if not t.exists():
                    return
                src = x_t[bass.ds(t.n, 1)].rearrange("a p n -> (a p) n")
                src_c = c_t[bass.ds(t.n, 1)].rearrange("a p n -> (a p) n")
                if t.at_least(2):
                    sp.wait_ge(x2_sb, t.n - 1)
                    sp.wait_ge(ctxT_ps, t.n - 1)
                sp.dma_start(x_sb[t.par][:], src).then_inc(x_in[t.par], 16)
                sp.dma_start(c_sb[t.par][:], src_c).then_inc(c_in[t.par], 16)

            def store(t):
                if not t.exists():
                    return
                sp.wait_ge(out_ready, t.n + 1)
                sp.dma_start(out_t[bass.ds(t.n, 1)].rearrange("a p n -> (a p) n"),
                             out_sb[t.par][:]).then_inc(stored[t.par], 16)

            sp.dma_start(x_sb[0][:], x_t[0]).then_inc(x_in[0], 16)
            sp.dma_start(cst[:], consts).then_inc(consts_in, 16)
            sp.dma_start(c_sb[0][:], c_t[0]).then_inc(c_in[0], 16)
            sp.dma_start(vec[:], vecs).then_inc(weights_in, 16)
            for dst, src in ((w_k, wk), (w_v, wv), (w_q, wq), (w_c, wc), (w_r, router), (w_s1, sw1)):
                sp.dma_start(dst[:], src).then_inc(weights_in, 16)
            sp.dma_start(w_s2[:], sw2.rearrange("(c p) o -> p c o", p=P)).then_inc(weights_in, 16)
            sp.dma_start(tab[:], tables).then_inc(weights_in, 16)
            sp.dma_start(x_sb[1][:], x_t[1]).then_inc(x_in[1], 16)
            sp.dma_start(c_sb[1][:], c_t[1]).then_inc(c_in[1], 16)
            sp.wait_ge(setup, 1)
            sp.dma_start(rows_dram[PAD_ROW:PAD_ROW + TILE].rearrange("(p s) n -> p (s n)", s=SUB),
                         pad[:]).then_inc(pads_in, 16)
            sp.dma_start(out[TOKENS:OUT_ROWS].rearrange("(p s) n -> p s n", s=SUB),
                         pad[:, :, 0:D]).then_inc(dummies_in, 16)

            def step(t):
                store(t.later(-2))
                if t.exists():
                    load(t.later(2))

            pipeline(sp, step)

            def load_rows(i, u):
                row = sp.value_load(row_of[0:1, bass.ds(i * DEEP + u, 1)], min_val=0, max_val=PAD_ROW)
                sp.dma_start(xb[u][:], rows_dram[bass.ds(row, TILE)].rearrange("(p s) n -> p (s n)", s=SUB)
                             ).then_inc(xb_in[u], 16)

            def load_weights(i, u):
                e = sp.value_load(expert_of[0:1, bass.ds(i * DEEP + u, 1)], min_val=0, max_val=E - 1)
                if not isinstance(i, int) or i > 0:
                    sp.wait_ge(byT_sb, (i - 1) * DEEP + u + 1)
                sp.dma_start(w1b[u][:], ew1[bass.ds(e, 1)].rearrange("a p n -> (a p) n")
                             ).then_inc(wb_in[u], 16)
                sp.dma_start(w2b[u][:], ew2[bass.ds(e, 1)].rearrange("a (c p) n -> p (a c) n", p=P)
                             ).then_inc(wb_in[u], 16)
                sp.dma_start(exb[u][:], extra[bass.ds(e, 1)].rearrange("a p n -> (a p) n")
                             ).then_inc(wb_in[u], 16)

            def expert_load(i, u):
                load_weights(i, u)
                load_rows(i, u)

            sp.wait_ge(table_done, 1)
            for u in range(DEEP):
                load_weights(0, u)
            for e in range(E):
                at = sp.value_load(pad_at[0:1, e:e + 1], min_val=e * REGION, max_val=e * REGION + TOKENS)
                sp.dma_start(rows_dram[bass.ds(at, TILE)].rearrange("(p s) n -> p (s n)", s=SUB),
                             pad[:]).then_inc(pads_in, 16)
            sp.wait_ge(pads_in, 16 * (E + 1))
            for k in range(2):
                sp.wait_ge(scattered[k], SCAT_ALL)
            for u in range(DEEP):
                load_rows(0, u)
            with sp.Fori(1, XTILES // DEEP) as i:
                for u in range(DEEP):
                    expert_load(i, u)
            sp.wait_ge(added, 16 * SUB * XTILES)

        @block.tensor
        def _(pe):
            mm, tr = nc.tensor.matmul, nc.tensor.transpose
            pe.wait_ge(consts_in, 16)
            pe.wait_ge(weights_in, 16 * 9)

            def turn(dst, src, width=D):
                for s in range(SUB):
                    last = tr(dst[:, s * P:(s + 1) * P], src(s), ident)
                return last

            def step(t):
                u, v = t.later(-1), t.later(-2)
                has_u, has_v = u.exists(), v.exists()

                def hidden(c):
                    mm(ps_h[c][:], w_s1[:, c * P:(c + 1) * P], nT[v.par][:], start=True, stop=True
                       ).then_inc(h_ps, 1)

                if not t.exists() and not has_u and has_v:
                    pe.wait_ge(routed, v.n + 1)
                    pe.wait_ge(seen_sb, v.n)
                    mm(ps_count, ones_b[:], seen[:], start=True, stop=False, skip_group_check=True)
                    for s in range(SUB):
                        last = mm(ps_count, ones_b[:], chosen[:, s, :], start=False, stop=(s == SUB - 1),
                                  skip_group_check=True)
                    last.then_inc(count_ps, 1)
                if has_v:
                    pe.wait_ge(routed, v.n + 1)
                    every = chosen[:].rearrange("p s e -> p (s e)")
                    by_sub = ps_rank.rearrange("p (s e) -> p s e", s=SUB)
                    mm(ps_rank, before_b[:], every, start=True, stop=False)
                    for s in range(SUB - 1):
                        mm(by_sub[:, s + 1:SUB, :], ones_b[:],
                           chosen[:, s:s + 1, :].to_broadcast([P, SUB - 1 - s, E]),
                           start=False, stop=False, skip_group_check=True)
                    if v.at_least(1):
                        pe.wait_ge(seen_sb, v.n)
                    mm(by_sub, ones_b[:], seen[:].unsqueeze(1).to_broadcast([P, SUB, E]),
                       start=False, stop=True).then_inc(rank_ps, 1)
                if t.exists():
                    pe.wait_ge(c_in[t.par], 16 * (t.half + 1))
                    if t.at_least(1):
                        pe.wait_ge(projT_sb, t.n)
                    turn(ps_ctxT, lambda s: c_sb[t.par][:, s, :]).then_inc(ctxT_ps, 1)
                    pe.wait_ge(xn_sb, t.n + 1)
                    if t.at_least(1):
                        pe.wait_ge(x2_sb, t.n)
                    turn(ps_xT, lambda s: xn[:, s, :]).then_inc(xT_ps, 1)
                if has_v:
                    pe.wait_ge(nT_sb, v.n + 1)
                    if v.at_least(1):
                        pe.wait_ge(out_ready, v.n)
                    hidden(0)
                if t.exists():
                    pe.wait_ge(ctxT_sb, t.n + 1)
                    mm(ps_k[:], w_k[:], ctxT[:], start=True, stop=True).then_inc(k_ps, 1)
                    pe.wait_ge(xnT_sb, t.n + 1)
                    mm(ps_q[:], w_q[:], xnT[:], start=True, stop=True).then_inc(q_ps, 1)
                    mm(ps_v[:], w_v[:], ctxT[:], start=True, stop=True).then_inc(v_ps, 1)
                    pe.wait_ge(kT_sb, t.n + 1)
                    mm(ps_csum[:], heads, kT[:], start=True, stop=True).then_inc(csum_ps, 1)
                if has_v:
                    if not t.exists():
                        pe.wait_ge(x2_sb, TILES)
                    hidden(1)
                    hidden(2)
                    pe.wait_ge(h_sb, v.n * HC + 1)
                if has_u:
                    pe.wait_ge(rows_sb, u.n + 1)
                    turn(ps_nT, lambda s: rows[u.par][:, s, 0:D]).then_inc(nT_ps, 1)
                if has_v:
                    if t.exists():
                        pe.wait_ge(k_parts, t.n + 1)
                    hidden(3)
                if has_u:
                    pe.wait_ge(nT_sb, u.n + 1)
                    if u.at_least(1):
                        pe.wait_ge(place_sb, u.n)
                    for s in range(SUB):
                        last = mm(ps_logit[:, s * E:(s + 1) * E], nT[u.par][:, s * P:(s + 1) * P], w_r[:],
                                  start=True, stop=True)
                    last.then_inc(logit_ps, 1)
                if has_v:
                    if t.exists():
                        pe.wait_ge(q_parts, t.n + 1)
                    for c in range(HC):
                        pe.wait_ge(h_sb, v.n * HC + c + 1)
                        last = mm(ps_yT[:], w_s2[:, c, :], hT[:, c, :], start=(c == 0), stop=(c == HC - 1))
                    last.then_inc(yT_ps, 1)
                if t.exists():
                    pe.wait_ge(attn_sb, t.n + 1)
                    mm(ps_projT[:], w_c[:], attnT[:], start=True, stop=True).then_inc(projT_ps, 1)
                if has_v:
                    pe.wait_ge(yT_sb, v.n + 1)
                    turn(ps_y, lambda s: yT[:, s * P:(s + 1) * P]).then_inc(y_ps, 1)
                if t.exists():
                    pe.wait_ge(projT_sb, t.n + 1)
                    turn(ps_proj, lambda s: projT[:, s * P:(s + 1) * P]).then_inc(proj_ps, 1)

            pipeline(pe, step)

            def turn_in(i, u):
                j = i * DEEP + u
                pe.wait_ge(xb_in[u], 16 * (i + 1))
                turn(pb_xT, lambda s: xb[u][:, s, 0:D]).then_inc(bxT_ps, 1)

            def turn_out(i, u):
                j = i * DEEP + u
                pe.wait_ge(byT_sb, j + 1)
                if not isinstance(i, int) or j > 0:
                    pe.wait_ge(by_sb, j)
                turn(pb_y, lambda s: yT[:, s * P:(s + 1) * P]).then_inc(by_ps, 1)

            def expert_step(i, u):
                j = i * DEEP + u
                first = isinstance(i, int) and j == 0
                last_tile = isinstance(i, int) and j == XTILES - 1
                if first:
                    pe.wait_ge(out_ready, TILES)
                    turn_in(i, u)
                pe.wait_ge(bxT_sb, j + 1)
                pe.wait_ge(wb_in[u], 16 * 3 * (i + 1))
                for c in range(HC):
                    mm(pb_h[c][:], w1b[u][:, c * P:(c + 1) * P], xnT[:], start=True, stop=True
                       ).then_inc(bh_ps, 1)
                if not first:
                    turn_out(i - (u == 0), (u - 1) % DEEP)
                if not last_tile:
                    turn_in(i + (u == DEEP - 1), (u + 1) % DEEP)
                for c in range(HC):
                    pe.wait_ge(bh_sb, j * HC + c + 1)
                    last = mm(pb_yT[:], w2b[u][:, c, :], hT[:, c, :], start=(c == 0), stop=(c == HC - 1))
                last.then_inc(byT_ps, 1)
                if last_tile:
                    turn_out(i, u)

            experts(pe, expert_step)

        @block.scalar
        def _(act):
            fn = nc.scalar.activation

            def feature(col):
                return vec[:, col:col + 1]

            def normalise(which, dst, src):
                for s in range(SUB):
                    last = fn(dst(s), src(s), ACT.Identity, bias=shift[which][:, s:s + 1],
                              scale=rstd[which][:, s:s + 1])
                return last

            def norm_x(t):
                if t.exists():
                    act.wait_ge(shift_sb[0], t.n + 1)
                    normalise(0, lambda s: xn[:, s, :], lambda s: x_sb[t.par][:, s, :]).then_inc(xn_sb, 1)

            act.wait_ge(weights_in, 16 * 9)
            norm_x(FIRST)

            def step(t):
                u, v = t.later(-1), t.later(-2)
                has_u, has_v = u.exists(), v.exists()

                def hidden(c):
                    act.wait_ge(h_ps, v.n * HC + c + 1)
                    fn(hT[:, c, :], ps_h[c][:], ACT.Relu, bias=feature(V_SB1 + c)).then_inc(h_sb, 1)

                if t.exists():
                    act.wait_ge(ctxT_ps, t.n + 1)
                    fn(ctxT[:], ps_ctxT[:], ACT.Copy).then_inc(ctxT_sb, 1)
                    act.wait_ge(xT_ps, t.n + 1)
                    fn(xnT[:], ps_xT[:], ACT.Copy).then_inc(xnT_sb, 1)
                if has_v:
                    hidden(0)
                if t.exists():
                    act.wait_ge(k_ps, t.n + 1)
                    fn(k_exp[:], ps_k[:], ACT.Exp, bias=feature(V_BK))
                    fn(k_lin[:], ps_k[:], ACT.Relu, bias=feature(V_BK)).then_inc(k_parts, 1)
                    act.wait_ge(q_ps, t.n + 1)
                    fn(q_exp[:], ps_q[:], ACT.Exp, bias=feature(V_BQ))
                    fn(q_lin[:], ps_q[:], ACT.Relu, bias=feature(V_BQ)).then_inc(q_parts, 1)
                if has_u:
                    act.wait_ge(shift_sb[1], u.n + 1)
                    if u.at_least(2):
                        act.wait_ge(scattered[u.par], 16 * SCATTERS * u.half)
                    normalise(1, lambda s: rows[u.par][:, s, 0:D], lambda s: x2[u.par][:, s, :]
                              ).then_inc(rows_sb, 1)
                if has_v:
                    hidden(1)
                    hidden(2)
                if has_u:
                    act.wait_ge(nT_ps, u.n + 1)
                    fn(nT[u.par][:], ps_nT[:], ACT.Identity, scale=feature(V_NW)).then_inc(nT_sb, 1)
                if has_v:
                    hidden(3)
                if has_u:
                    act.wait_ge(key_sb, u.n + 1)
                    fn(e_neg[:], key[:], ACT.Exp, scale=-1.0).then_inc(e_sb, 1)
                norm_x(t.later(1))
                if has_v:
                    act.wait_ge(yT_ps, v.n + 1)
                    fn(yT[:], ps_yT[:], ACT.Identity, bias=feature(V_SB2)).then_inc(yT_sb, 1)
                if t.exists():
                    act.wait_ge(projT_ps, t.n + 1)
                    fn(projT[:], ps_projT[:], ACT.Identity, bias=feature(V_BC)).then_inc(projT_sb, 1)

            pipeline(act, step)

            def expert_step(i, u):
                j = i * DEEP + u
                act.wait_ge(wb_in[u], 16 * 3 * (i + 1))
                for c in range(HC):
                    act.wait_ge(bh_ps, j * HC + c + 1)
                    fn(hT[:, c, :], pb_h[c][:], ACT.Relu, bias=exb[u][:, COL_B1 + c:COL_B1 + c + 1]
                       ).then_inc(bh_sb, 1)

            experts(act, expert_step)

        @block.gpsimd
        def _(pool):
            def scatter(t, which):
                for s in range(SUB):
                    pool.indirect_dma_start(
                        rows_dram, bass.IndirectOffsetOnAxis(ap=slot[t.par][:, which, s:s + 1], axis=0),
                        rows[t.par][:, s, :], None).then_inc(scattered[t.par], 16)

            def raise_power(which, t):
                pool.wait_ge(spread_sb[which], t.n + 1)
                nc.gpsimd.tensor_tensor(rstd[which][:], spread[which][:], minus_half[:], ALU.pow
                                        ).then_inc(power[which], 1)
                pool.wait_ge(power[which], t.n + 1)
                nc.gpsimd.tensor_tensor(shift[which][:], neg_mean[which][:], rstd[which][:], ALU.mult
                                        ).then_inc(shift_sb[which], 1)

            pool.wait_ge(setup, 1)
            raise_power(0, FIRST)

            def step(t):
                v = t.later(-2)
                has_v = v.exists()
                if has_v:
                    pool.wait_ge(slot_sb, v.n + 1)
                    pool.wait_ge(routed, v.n + 1)
                    pool.wait_ge(rows_sb, v.n + 1)
                    carry_wait_pool(v.n)
                    scatter(v, 0)
                if t.exists():
                    pool.wait_ge(qT_sb, t.n + 1)
                    pool.wait_ge(kT_sb, t.n + 1)
                    nc.gpsimd.tensor_tensor(qk[:], qT[:], kT[:], ALU.mult).then_inc(qk_sb, 1)
                if t.later(1).exists():
                    raise_power(0, t.later(1))
                if has_v:
                    scatter(v, 1)
                if t.exists():
                    raise_power(1, t)

            pipeline(pool, step)
            for k in range(2):
                pool.wait_ge(stored[k], 16 * TILES // 2)
            pool.wait_ge(dummies_in, 16)

            def expert_step(i, u):
                j = i * DEEP + u
                pool.wait_ge(by_sb, j + 1)
                if not isinstance(i, int) or j > 0:
                    pool.wait_ge(added, 16 * SUB * j)
                carry_wait_pool(TILES + j)
                for s in range(SUB):
                    pool.indirect_dma_start(
                        out, bass.IndirectOffsetOnAxis(ap=tok[u][:, s:s + 1], axis=0),
                        yb[u][:, s, :], None, compute_op=ALU.add).then_inc(added, 16)

            experts(pool, expert_step)

        @block.vector
        def _(dve):
            v_ = nc.vector

            def feature(col):
                return vec[:, col:col + 1]

            class Steps:

                def __init__(self, sem, n, per):
                    self.sem, self.start, self.k = sem, n * per, 0

                def then(self, ins):
                    ins.then_inc(self.sem, 1)
                    self.k += 1

                def wait(self):
                    dve.wait_ge(self.sem, self.start + self.k)

            STAT_STEPS = 2

            def statistics(which, t, src):
                c = Steps(stat[which], t.n, STAT_STEPS)
                for s in range(SUB):
                    last = v_.bn_stats(st[which][:, s, :], src[:, s, :])
                c.then(last)
                c.wait()
                carry_wait_dve()
                for s in range(SUB):
                    last = v_.bn_aggr(mv[which][:, s, :], st[which][:, s, :])
                c.then(last)
                c.wait()
                if t.at_least(1):
                    dve.wait_ge(shift_sb[which], t.n)
                v_.tensor_scalar(neg_mean[which][:], mv[which][:, :, 0], -1.0, None, ALU.mult)
                if which == 0:
                    scale, eps = 1.0, LN_EPS
                else:
                    scale, eps = 1.0 + RMS_EPS, LN_EPS * RMS_EPS
                v_.tensor_scalar(spread[which][:], mv[which][:, :, 1], scale, eps, ALU.mult, ALU.add
                                 ).then_inc(spread_sb[which], 1)

            def stats_x(t):
                if t.exists():
                    dve.wait_ge(x_in[t.par], 16 * (t.half + 1))
                    statistics(0, t, x_sb[t.par])

            dve.wait_ge(consts_in, 16)
            v_.memset(minus_half[:], -0.5)
            v_.memset(seen[:], 0.0)
            v_.memset(score[:, :, E:E + 1], COMB_EPS)
            v_.tensor_copy(before_b[:], cst[:, CM_BEFORE:CM_BEFORE + P])
            v_.tensor_copy(ones_b[:], cst[:, CM_ONES:CM_ONES + P])
            v_.memset(pad[:, :, 0:COL_ID], 0.0)
            v_.memset(pad[:, :, COL_ID + 1:ROW], 0.0)
            for k in range(2):
                v_.memset(rows[k][:, :, COL_ID + 1:ROW], 0.0)
            v_.tensor_scalar(rows[1][:, :, COL_ID], id0, float(-TILE), None, ALU.add)
            v_.tensor_scalar(pad[:, :, COL_ID], id0, float(TOKENS), None, ALU.add).then_inc(setup, 1)
            dve.wait_ge(setup, 1)
            stats_x(FIRST)
            dve.wait_ge(weights_in, 16 * 9)

            def over_experts(ap):
                return ap.unsqueeze(2).to_broadcast([P, SUB, E])

            ROUTE_STEPS = 10

            def route_tile(u):
                start = u.n * ROUTE_STEPS

                def done(ins):
                    ins.then_inc(route, 1)

                def wait(k):
                    dve.wait_ge(route, start + k)

                dve.wait_ge(key_sb, u.n + 1)
                carry_wait_dve()
                for s in range(SUB):
                    last = v_.max(sorted_key[:, s, :], key[:, s, :])
                done(last)
                wait(1)
                carry_wait_dve()
                for s in range(SUB):
                    last = v_.max_index(sorted_at[:, s, :], sorted_key[:, s, :], key[:, s, :])
                done(last)
                dve.wait_ge(e_sb, u.n + 1)
                done(v_.tensor_scalar(den[:], e_neg[:], 1.0, None, ALU.add))
                wait(2)
                done(v_.tensor_copy(top_at[:], sorted_at[:, :, 0:TOPK]))
                wait(3)
                done(v_.reciprocal(prob[:], den[:]))
                wait(4)
                four = [P, SUB, TOPK, E]
                done(v_.tensor_tensor(hot[:].rearrange("p i s e -> p s i e"),
                                      top_at[:].unsqueeze(3).to_broadcast(four),
                                      expert_no.unsqueeze(1).unsqueeze(1).to_broadcast(four), ALU.is_equal))
                wait(6)
                if u.at_least(1):
                    dve.wait_ge(rank_ps, u.n)
                done(v_.tensor_tensor(chosen[:], hot[:, 0], hot[:, 1], ALU.add))
                wait(7)
                done(v_.tensor_tensor(score[:, :, 0:E], prob[:], chosen[:], ALU.mult))
                wait(8)
                done(v_.tensor_reduce(total[:], score[:], AX, ALU.add))
                wait(9)
                done(v_.reciprocal(inv_total[:], total[:]))
                wait(10)
                if u.at_least(2):
                    dve.wait_ge(scattered[u.par], 16 * SCATTERS * u.half)
                v_.tensor_tensor(rows[u.par][:, :, COL_W:COL_W + E], score[:, :, 0:E],
                                 inv_total[:].unsqueeze(2).to_broadcast([P, SUB, E]), ALU.mult)
                v_.tensor_scalar(rows[u.par][:, :, COL_ID], rows[1 - u.par][:, :, COL_ID], float(TILE), None,
                                 ALU.add).then_inc(routed, 1)

            def count_tile(v):
                v_.tensor_reduce(tile_count[:], chosen[:].rearrange("p s e -> p e s"), AX, ALU.add
                                 ).then_inc(counted, 1)

            def step(t):
                u, v = t.later(-1), t.later(-2)
                has_u, has_v = u.exists(), v.exists()
                if has_v:
                    dve.wait_ge(rank_ps, v.n + 1)
                    dve.wait_ge(routed, v.n + 1)
                    v_.tensor_tensor(place[:], ps_rank.rearrange("p (s e) -> p s e", s=SUB), base, ALU.add
                                     ).then_inc(place_sb, 1)
                    count_tile(v)
                    dve.wait_ge(place_sb, v.n + 1)
                    v_.tensor_tensor(placed[:], hot[:], place[:].unsqueeze(1).to_broadcast([P, TOPK, SUB, E]),
                                     ALU.mult).then_inc(placed_sb, 1)
                    dve.wait_ge(counted, v.n + 1)
                    v_.tensor_tensor(seen[:], seen[:], tile_count[:], ALU.add).then_inc(seen_sb, 1)
                    dve.wait_ge(placed_sb, v.n + 1)
                    v_.tensor_reduce(slot_f[:], placed[:], AX, ALU.add).then_inc(slot_f_sb, 1)
                    dve.wait_ge(slot_f_sb, v.n + 1)
                    if v.at_least(2):
                        dve.wait_ge(scattered[v.par], 16 * SCATTERS * v.half)
                    v_.tensor_copy(slot[v.par][:], slot_f[:]).then_inc(slot_sb, 1)
                if t.exists():
                    dve.wait_ge(k_parts, t.n + 1)
                    v_.scalar_tensor_tensor(kT[:], k_exp[:], 1.0, k_lin[:], ALU.min, ALU.add
                                            ).then_inc(kT_sb, 1)
                stats_x(t.later(1))
                if t.exists():
                    dve.wait_ge(q_parts, t.n + 1)
                    v_.scalar_tensor_tensor(qT[:], q_exp[:], 1.0, q_lin[:], ALU.min, ALU.add
                                            ).then_inc(qT_sb, 1)
                    dve.wait_ge(csum_ps, t.n + 1)
                    v_.reciprocal(k_inv[:], ps_csum[:]).then_inc(inv_sb, 1)
                if has_u:
                    dve.wait_ge(logit_ps, u.n + 1)
                    v_.tensor_scalar(key[:], ps_logit.rearrange("p (s e) -> p s e", s=SUB), SIG_ONE, SIG_ZERO,
                                     ALU.min, ALU.max).then_inc(key_sb, 1)
                if t.exists():
                    dve.wait_ge(inv_sb, t.n + 1)
                    dve.wait_ge(qk_sb, t.n + 1)
                    v_.tensor_tensor(qkn[:], qk[:], k_inv[:], ALU.mult).then_inc(qkn_sb, 1)
                    dve.wait_ge(qkn_sb, t.n + 1)
                    dve.wait_ge(v_ps, t.n + 1)
                    v_.scalar_tensor_tensor(attnT[:], ps_v[:], feature(V_BV), qkn[:], ALU.add, ALU.mult
                                            ).then_inc(attn_sb, 1)
                if has_u:
                    route_tile(u)
                if has_v:
                    dve.wait_ge(y_ps, v.n + 1)
                    if v.at_least(2):
                        dve.wait_ge(stored[v.par], 16 * v.half)
                    v_.tensor_tensor(out_sb[v.par][:].rearrange("p s d -> p (s d)"), ps_y[:],
                                     x2[v.par][:].rearrange("p s d -> p (s d)"), ALU.add).then_inc(out_ready, 1)
                if t.exists():
                    dve.wait_ge(proj_ps, t.n + 1)
                    if has_v:
                        dve.wait_ge(out_ready, v.n + 1)
                    v_.tensor_tensor(x2[t.par][:].rearrange("p s d -> p (s d)"), ps_proj[:],
                                     x_sb[t.par][:].rearrange("p s d -> p (s d)"), ALU.add).then_inc(x2_sb, 1)
                    dve.wait_ge(x2_sb, t.n + 1)
                    statistics(1, t, x2[t.par])
                if not t.exists() and not has_u and has_v:
                    make_table()

            def make_table():
                c = Steps(table, 0, 0)

                def do(ins):
                    c.then(ins)
                    c.wait()

                step_t = tab[:, TB_STEP:TB_UPTO].rearrange("a (e m) -> a e m", e=E)
                upto_t = tab[:, TB_UPTO:TB_TILE].rearrange("a (e m) -> a e m", e=E)
                tile_t, reg_t = tab[:, TB_TILE:TB_REG], tab[:, TB_REG:TB_REG + E]
                dve.wait_ge(count_ps, 1)
                do(v_.tensor_copy(cnt[:], ps_count[0:1, :]))
                v_.tensor_tensor(pad_at[:], cnt[:], reg_t, ALU.add)
                do(v_.tensor_tensor(tl_a[:], cnt[:].unsqueeze(2).to_broadcast([1, E, TILES]), step_t, ALU.is_gt))
                do(v_.tensor_reduce(tl_n[:], tl_a[:], AX, ALU.add))
                do(v_.tensor_tensor(tl_b[:], tl_n[:].unsqueeze(1).to_broadcast([1, E, E]), upto_t, ALU.mult))
                do(v_.tensor_reduce(tl_end[:], tl_b[:], AX, ALU.add))
                many = [1, XTILES, E]
                do(v_.tensor_tensor(tl_past[:], tile_t.unsqueeze(2).to_broadcast(many),
                                    tl_end[:].unsqueeze(1).to_broadcast(many), ALU.is_ge))
                do(v_.tensor_reduce(tl_e[:], tl_past[:], AX, ALU.add))
                do(v_.tensor_tensor(tl_used[:], tl_past[:], tl_n[:].unsqueeze(1).to_broadcast(many), ALU.mult))
                do(v_.tensor_reduce(tl_first[:], tl_used[:], AX, ALU.add))
                do(v_.tensor_tensor(tl_k[:], tile_t, tl_first[:], ALU.subtract))
                do(v_.tensor_scalar(tl_base[:], tl_e[:], float(REGION), None, ALU.mult))
                do(v_.scalar_tensor_tensor(tl_row[:], tl_k[:], float(TILE), tl_base[:], ALU.mult, ALU.add))
                do(v_.tensor_scalar(expert_of[:], tl_e[:], float(E - 1), None, ALU.min))
                v_.tensor_scalar(row_of[:], tl_row[:], float(PAD_ROW), None, ALU.min).then_inc(table_done, 1)

            pipeline(dve, step)

            def finish(i, u):
                j = i * DEEP + u
                dve.wait_ge(by_ps, j + 1)
                dve.wait_ge(w_sb, j + 1)
                for s in range(SUB):
                    last = v_.tensor_scalar(yb[u][:, s, :], pb_y[:, s * P:(s + 1) * P], w_row[:, s:s + 1], None,
                                            ALU.mult)
                last.then_inc(by_sb, 1)

            def turned(i, u):
                j = i * DEEP + u
                dve.wait_ge(bxT_ps, j + 1)
                v_.tensor_scalar(xnT[:], pb_xT[:], feature(V_NW), None, ALU.mult).then_inc(bxT_sb, 1)

            def expert_step(i, u):
                j = i * DEEP + u
                first = isinstance(i, int) and j == 0
                last_tile = isinstance(i, int) and j == XTILES - 1
                if first:
                    turned(i, u)
                else:
                    finish(i - (u == 0), (u - 1) % DEEP)
                if not last_tile:
                    turned(i + (u == DEEP - 1), (u + 1) % DEEP)
                dve.wait_ge(xb_in[u], 16 * (i + 1))
                dve.wait_ge(wb_in[u], 16 * 3 * (i + 1))
                v_.tensor_tensor(w_pick[:], xb[u][:, :, COL_W:COL_W + E],
                                 exb[u][:, COL_HOT:COL_HOT + E].unsqueeze(1).to_broadcast([P, SUB, E]), ALU.mult
                                 ).then_inc(pick_sb, 1)
                if not isinstance(i, int) or i > 0:
                    dve.wait_ge(added, 16 * SUB * (j - DEEP + 1))
                v_.tensor_copy(tok[u][:], xb[u][:, :, COL_ID])
                dve.wait_ge(pick_sb, j + 1)
                if not first:
                    dve.wait_ge(by_sb, j)
                v_.tensor_reduce(w_row[:], w_pick[:], AX, ALU.add).then_inc(w_sb, 1)
                dve.wait_ge(byT_ps, j + 1)
                v_.tensor_scalar(yT[:], pb_yT[:], exb[u][:, COL_B2:COL_B2 + 1], None, ALU.add
                                 ).then_inc(byT_sb, 1)
                if last_tile:
                    finish(i, u)

            experts(dve, expert_step)


def kernel(**inputs):
    import concourse.bacc as bacc
    from concourse.bass_utils import run_bass_kernel_spmd

    def given(name):
        return np.asarray(inputs[name])

    ffn, att = "L0_ffn_", "L0_xattn_"
    consts, tables = constants()
    columns = [given(att + n)[:, None] for n in ("wq_b", "wk_b", "wv_b", "wc_b")]
    columns += [given(ffn + "norm_weight")[:, None], given(ffn + "sb1").reshape(HC, P).T, given(ffn + "sb2")[:, None]]
    hot = np.broadcast_to(np.eye(E, dtype=np.float32)[:, None, :], (E, P, E))
    extra = np.concatenate([given(ffn + "eb1").reshape(E, HC, P).transpose(0, 2, 1),
                            given(ffn + "eb2")[:, :, None], hot], axis=2)
    arrays = {
        "x": given("x").reshape(TOKENS, D),
        "ctx_in": given("ctx_1024").reshape(TOKENS, D),
        "wq": given(att + "wq_w"), "wk": given(att + "wk_w"), "wv": given(att + "wv_w"), "wc": given(att + "wc_w"),
        "vecs": np.concatenate(columns, axis=1),
        "router": given(ffn + "router_w").T,
        "sw1": given(ffn + "sw1"), "sw2": given(ffn + "sw2"),
        "ew1": given(ffn + "ew1"), "ew2": given(ffn + "ew2"),
        "extra": extra, "consts": consts, "tables": tables,
    }
    arrays = {name: np.ascontiguousarray(a) for name, a in arrays.items()}
    nc = bacc.Bacc("TRN2", target_bir_lowering=False, num_devices=1)
    aps = {name: nc.dram_tensor(name, a.shape, mybir.dt.from_np(a.dtype), kind="ExternalInput").ap()
           for name, a in arrays.items()}
    rows_dram = nc.dram_tensor("rows_dram", (X_ROWS, ROW), F32, kind="Internal").ap()
    out = nc.dram_tensor("out", (OUT_ROWS, D), F32, kind="ExternalOutput").ap()
    token_kernel(nc, **aps, rows_dram=rows_dram, out=out)
    result = run_bass_kernel_spmd(nc, [arrays], core_ids=[0]).results[0]["out"]
    return result[:TOKENS].reshape(128, 64, D)
```

```python
from contextlib import ExitStack

import numpy as np

import concourse.bass as bass
from concourse import mybir

F32 = mybir.dt.float32
F32R = mybir.dt.float32r
BF16 = mybir.dt.bfloat16
I32 = mybir.dt.int32
U32 = mybir.dt.uint32
ALU = mybir.AluOpType
ACT = mybir.ActivationFunctionType
AX = mybir.AxisListType.X

P = 128
D = 128
HID = 512
HC = HID // P
E = 8
TOPK = 2
HEADS, DEPTH = 16, 8
TOKENS = 128 * 64
SUB = 4
TILE = P * SUB
TILES = TOKENS // TILE
LN_EPS = 1e-5
RMS_EPS = 1e-8
COMB_EPS = 1e-6
SIG_ONE, SIG_ZERO = 16.635532, -88.0

COL_W, COL_ID, ROW = D, D + E, 140
REGION = TOKENS + TILE
PAD_ROW = E * REGION
X_ROWS = PAD_ROW + TILE
XTILES = TOPK * TOKENS // TILE + E - 1
OUT_ROWS = TOKENS + TILE
COL_B1, COL_B2, COL_HOT, EXTRA = 0, HC, HC + 1, HC + 1 + E
CM_IDENT, CM_BEFORE, CM_ONES, CM_HEADS = 0, P, 2 * P, 3 * P
CS_BASE, CS_EXPERT, CS_ID = 4 * P, 4 * P + SUB * E, 4 * P + SUB * E + E
CS_WHOLE = CS_ID + SUB
CS_SIGN = CS_WHOLE + 1
CONSTS = CS_SIGN + 1
TB_STEP, TB_UPTO, TB_TILE, TB_REG = 0, E * TILES, E * TILES + E * E, E * TILES + E * E + XTILES
TABLES = TB_REG + E
V_BQ, V_BK, V_BV, V_NW, V_SB1 = 0, 1, 2, 3, 4
VECS = V_SB1 + HC


def constants():
    c = np.zeros((P, CONSTS), np.float32)
    i = np.arange(P)
    c[:, CM_IDENT:CM_IDENT + P] = np.eye(P)
    c[:, CM_BEFORE:CM_BEFORE + P] = i[:, None] < i[None, :]
    c[:, CM_ONES:CM_ONES + P] = 1
    same_place = i[:, None] % DEPTH == i[None, :] % DEPTH
    c[:, CM_HEADS:CM_HEADS + P] = same_place & (i[:, None] // DEPTH <= i[None, :] // DEPTH)
    c[:, CS_BASE:CS_BASE + SUB * E] = np.tile(np.arange(E) * REGION, SUB)
    c[:, CS_EXPERT:CS_EXPERT + E] = np.arange(E)
    c[:, CS_ID:CS_ID + SUB] = np.arange(TILE).reshape(P, SUB)
    c[1, CS_WHOLE] = 1
    c[0, CS_SIGN], c[1, CS_SIGN] = 1, -1
    t = np.zeros((1, TABLES), np.float32)
    t[0, TB_STEP:TB_UPTO] = np.tile(np.arange(TILES) * TILE, E)
    t[0, TB_UPTO:TB_TILE] = (np.arange(E)[None, :] <= np.arange(E)[:, None]).ravel()
    t[0, TB_TILE:TB_REG] = np.arange(XTILES)
    t[0, TB_REG:] = np.arange(E) * REGION
    return c, t


class Tile:

    def __init__(self, group, offset, period=2, tiles=TILES):
        self.group, self.offset, self.period, self.tiles = group, offset, period, tiles
        self.static = isinstance(group, int)
        self.par = offset % period
        self.half = group + offset // period
        self.n = group * period + offset

    def later(self, k):
        return Tile(self.group, self.offset + k, self.period, self.tiles)

    def at_least(self, k):
        return not self.static or self.n >= k

    def exists(self):
        return not self.static or 0 <= self.n < self.tiles


def token_kernel(nc, x, ctx_in, wq, wk, wv, wc, vecs, bias_rows, router, sw1, sw2, ew1, ew2, extra, consts, tables,
                 rows_dram, out):
    with ExitStack() as stack:
        def sb(name, shape, dt=F32):
            return stack.enter_context(nc.sbuf_tensor("sb_" + name, shape, dt))

        def bank(name):
            return stack.enter_context(nc.psum_tensor("ps_" + name, [P, TILE], F32))

        def sem(name):
            return stack.enter_context(nc.semaphore(name))

        def pair_of(make, name):
            return [make(f"{name}{k}") for k in range(2)]

        cst = sb("cst", [P, CONSTS])
        tab = sb("tab", [1, TABLES])
        vec = sb("vec", [P, VECS])
        bias_in, bias_share, bias_hi = (sb(n, [2, 2, TILE], dt) for n, dt in
                                        (("bias_in", F32), ("bias_share", F32), ("bias_hi", F32R)))
        bias_parts, ones_r = sb("bias_parts", [2, 2, TILE], F32R), sb("ones_r", [2, P], F32R)
        w_q, w_k, w_v, w_c = (sb(n, [P, D]) for n in ("w_q", "w_k", "w_v", "w_c"))
        w_r = sb("w_r", [P, E])
        w_s1 = sb("w_s1", [P, HID])
        w_s2 = sb("w_s2", [P, HC, D])
        x_sb = [sb(f"x{k}", [P, SUB, D]) for k in range(2)]
        c_sb = [sb(f"c{k}", [P, SUB, D]) for k in range(2)]
        xn = sb("xn", [P, SUB, D])
        xnT, ctxT = sb("xnT", [P, TILE]), sb("ctxT", [P, TILE])
        k_exp, k_lin, q_exp, q_lin = (sb(n, [P, TILE]) for n in ("k_exp", "k_lin", "q_exp", "q_lin"))
        kT, qT = sb("kT", [P, TILE]), sb("qT", [P, TILE])
        k_inv, qk, qkn, attnT = (sb(n, [P, TILE]) for n in ("k_inv", "qk", "qkn", "attnT"))
        x2 = [sb(f"x2_{k}", [P, SUB, D]) for k in range(2)]
        rows = [sb(f"rows{k}", [P, SUB, ROW]) for k in range(2)]
        nT = sb("nT", [P, TILE])
        HI, LO = 0, 1
        ns = [[sb(f"n{part}{k}", [P, TILE], F32R) for part in "hl"] for k in range(2)]
        ws1 = [sb(f"ws1{part}", [P, HID], F32R) for part in "hl"]
        hT = sb("hT", [P, HC, TILE])
        yT = sb("yT", [P, TILE])
        out_sb = [sb(f"out{k}", [P, SUB, D]) for k in range(2)]
        pad = sb("pad", [P, SUB, ROW])
        st = [sb(f"st{k}", [P, SUB, 6]) for k in range(2)]
        mv = [sb(f"mv{k}", [P, SUB, 2]) for k in range(2)]
        spread = [sb(f"spread{k}", [P, SUB]) for k in range(2)]
        neg_mean = [sb(f"neg_mean{k}", [P, SUB]) for k in range(2)]
        rstd = [sb(f"rstd{k}", [P, SUB]) for k in range(2)]
        shift = [sb(f"shift{k}", [P, SUB]) for k in range(2)]
        carried = sb("carried", [P, 2])
        minus_half = sb("minus_half", [P, SUB])
        key, e_neg, den, prob = (sb(n, [P, SUB, E]) for n in ("key", "e_neg", "den", "prob"))
        sorted_key, sorted_at = sb("sorted_key", [P, SUB, E]), sb("sorted_at", [P, SUB, E], U32)
        hot = sb("hot", [P, TOPK, SUB, E])
        chosen = sb("chosen", [P, SUB, E], BF16)
        tile_count, seen = sb("tile_count", [P, E]), sb("seen", [P, E], BF16)
        before_b, ones_b = sb("before_b", [P, P], BF16), sb("ones_b", [P, P], BF16)
        score = sb("score", [P, SUB, E + 1])
        total, inv_total = sb("total", [P, SUB]), sb("inv_total", [P, SUB])
        place = sb("place", [P, SUB, E])
        placed = sb("placed", [P, TOPK, SUB, E])
        slot_f = sb("slot_f", [P, TOPK, SUB])
        slot = [sb(f"slot{k}", [P, TOPK, SUB], I32) for k in range(2)]
        DEEP = 3
        cnt = sb("cnt", [1, 2 * E])
        tl_whole, tl_whole_n, tl_start, tl_stop = (sb(n, s) for n, s in (
            ("tl_whole", [1, E, TILES]), ("tl_whole_n", [1, E]), ("tl_start", [1, E]), ("tl_stop", [1, E])))
        tl_from, tl_to, tl_in, tl_early = (sb(n, s) for n, s in (
            ("tl_from", [1, DEEP, E]), ("tl_to", [1, DEEP, E]), ("tl_in", [1, DEEP, E]), ("tl_early", [1, DEEP])))
        need_pads, need_rows = sb("need_pads", [1, DEEP], I32), sb("need_rows", [1, DEEP], I32)
        tl_a, tl_n = sb("tl_a", [1, E, TILES]), sb("tl_n", [1, E])
        tl_b, tl_end = sb("tl_b", [1, E, E]), sb("tl_end", [1, E])
        tl_past, tl_used = sb("tl_past", [1, XTILES, E]), sb("tl_used", [1, XTILES, E])
        tl_e, tl_first = sb("tl_e", [1, XTILES]), sb("tl_first", [1, XTILES])
        tl_k, tl_base, tl_row = (sb(n, [1, XTILES]) for n in ("tl_k", "tl_base", "tl_row"))
        row_of, expert_of = sb("row_of", [1, XTILES], I32), sb("expert_of", [1, XTILES], I32)
        pad_at = sb("pad_at", [1, E], I32)
        xb = [sb(f"xb{k}", [P, SUB, ROW]) for k in range(DEEP)]
        w1b = [sb(f"w1b{k}", [P, HID]) for k in range(DEEP - 1)] + [q_lin]
        w2b = [sb(f"w2b{k}", [P, HC, D]) for k in range(DEEP)]
        exb = [sb(f"exb{k}", [P, EXTRA]) for k in range(DEEP)]
        yb = [m[:].rearrange("p (s d) -> p s d", s=SUB) for m in (k_exp, k_lin, q_exp)]
        tok = [sb(f"tok{k}", [P, SUB], I32) for k in range(DEEP)]
        w_pick, w_row = sb("w_pick", [P, SUB, E]), [sb(f"w_row{k}", [P, SUB]) for k in range(DEEP)]
        xs = [[sb(f"xs{part}{k}", [P, TILE], F32R) for part in "hl"] for k in range(DEEP)]
        w1s = [[sb(f"w1{part}{k}", [P, HID], F32R) for part in "hl"] for k in range(DEEP)]
        w2s = [[sb(f"w2{part}{k}", [P, HC, D], F32R) for part in "hl"] for k in range(DEEP)]
        hs = [[sb(f"h{part}{k}", [P, HC, TILE], F32R) for part in "hl"] for k in range(DEEP)]

        b = [bank(f"b{k}") for k in range(8)]
        ps_ctxT, ps_xT, ps_k, ps_v, ps_q, ps_csum = b[0], b[1], b[2], b[3], b[4], b[6]
        ps_proj, ps_nT, ps_y = b[6], b[5], b[4]
        ps_h = [b[5], b[0], b[1], b[2]]
        ps_logit, ps_rank = b[7][:, 0:SUB * E], b[7][:, 64:64 + SUB * E]
        ps_count = b[6][:, 0:2 * E]
        pb_xT, pb_h, pb_yT, pb_y = b[0], b[1:5], b[5], b[6]

        ident, heads = cst[:, CM_IDENT:CM_IDENT + P], cst[:, CM_HEADS:CM_HEADS + P]
        base = cst[:, CS_BASE:CS_BASE + SUB * E].rearrange("p (s e) -> p s e", s=SUB)
        expert_no = cst[:, CS_EXPERT:CS_EXPERT + E]
        id0 = cst[:, CS_ID:CS_ID + SUB]

        consts_in = sem("consts_in")
        attention_in, ffn_in = sem("attention_in"), sem("ffn_in")
        ATTENTION_IN, FFN_IN = 16 * 6, 16 * 4
        x_in, c_in = pair_of(sem, "x_in"), pair_of(sem, "c_in")
        setup = sem("setup")
        ctxT_ps, xT_ps, k_ps, v_ps, q_ps = (sem(n) for n in ("ctxT_ps", "xT_ps", "k_ps", "v_ps", "q_ps"))
        csum_ps, proj_ps = sem("csum_ps"), sem("proj_ps")
        bias_steps, bias_sb = sem("bias_steps"), sem("bias_sb")
        rank_ps, nT_ps, logit_ps = sem("rank_ps"), sem("nT_ps"), sem("logit_ps")
        h_ps, y_ps, count_ps = sem("h_ps"), sem("y_ps"), sem("count_ps")
        ctxT_sb, k_parts, q_parts = sem("ctxT_sb"), sem("k_parts"), sem("q_parts")
        xn_sb, rows_sb, e_sb = sem("xn_sb"), sem("rows_sb"), sem("e_sb")
        h_sb = sem("h_sb")
        xnT_sb, kT_sb, qT_sb = sem("xnT_sb"), sem("kT_sb"), sem("qT_sb")
        nT_sb, n_hi, n_lo = sem("nT_sb"), sem("n_hi"), sem("n_lo")
        ws1_hi, ws1_lo = sem("ws1_hi"), sem("ws1_lo")
        inv_sb, qk_sb, qkn_sb, attn_sb = sem("inv_sb"), sem("qk_sb"), sem("qkn_sb"), sem("attn_sb")
        place_sb, placed_sb, slot_f_sb, slot_sb = (sem(n) for n in ("place_sb", "placed_sb", "slot_f_sb", "slot_sb"))
        key_sb, routed, out_ready, x2_sb = sem("key_sb"), sem("routed"), sem("out_ready"), sem("x2_sb")
        counted, seen_sb = sem("counted"), sem("seen_sb")
        route = sem("route")
        ROUTE_STEPS, CHOSEN = 9, 6
        stat = [sem("stat1"), sem("stat2")]
        spread_sb = [sem("spread1"), sem("spread2")]
        power = [sem("power1"), sem("power2")]
        shift_sb = [sem("shift1"), sem("shift2")]
        stored = pair_of(sem, "stored")
        scattered = pair_of(sem, "scattered")
        SCATTERS = TOPK * SUB
        table = sem("table")
        table_done, pad_at_sb = sem("table_done"), sem("pad_at_sb")
        pads_in = sem("pads_in")
        dummies_in = sem("dummies_in")
        pool_carried = sem("pool_carried")
        xb_in = [sem(f"xb_in{k}") for k in range(DEEP)]
        w_in = [sem(f"w_in{k}") for k in range(DEEP)]
        exb_in = [sem(f"exb_in{k}") for k in range(DEEP)]
        bxT_ps, bh_ps, byT_ps, by_ps = sem("bxT_ps"), sem("bh_ps"), sem("byT_ps"), sem("by_ps")
        xs_hi, xs_lo = sem("xs_hi"), sem("xs_lo")
        w1_hi, w1_lo, w2_hi, w2_lo = sem("w1_hi"), sem("w1_lo"), sem("w2_hi"), sem("w2_lo")
        h_hi, h_lo = sem("h_hi"), sem("h_lo")
        byT_sb, by_sb = sem("byT_sb"), sem("by_sb")
        pick_sb, w_sb = sem("pick_sb"), sem("w_sb")
        added = sem("added")
        ADDED = 16 * SUB

        x_t = x.rearrange("(t p s) d -> t p (s d)", p=P, s=SUB)
        c_t = ctx_in.rearrange("(t p s) d -> t p (s d)", p=P, s=SUB)
        out_t = out.rearrange("(t p s) d -> t p (s d)", p=P, s=SUB)
        FIRST = Tile(0, 0)
        SCAT_ALL = 16 * SCATTERS * TILES // 2

        def pipeline(engine, step):
            for t in range(4):
                step(Tile(0, t))
            with engine.Fori(2, TILES // 2 - 1) as pair:
                step(Tile(pair, 0))
                step(Tile(pair, 1))
            for t in range(TILES - 2, TILES + 2):
                step(Tile(0, t))

        def experts(engine, step, drain):
            for k in range(2 * DEEP):
                step(Tile(0, k, DEEP, XTILES))
            with engine.Fori(2, XTILES // DEEP - 1) as group:
                for k in range(DEEP):
                    step(Tile(group, k, DEEP, XTILES))
            for k in range(XTILES - DEEP, XTILES + drain):
                step(Tile(0, k, DEEP, XTILES))

        assert XTILES % DEEP == 0
        XFIRST = Tile(0, 0, DEEP, XTILES)

        def carry_wait_dve():
            nc.vector.memset(carried[:, 1:2], 0.0)

        def carry_wait_pool(earlier):
            if not isinstance(earlier, int) or earlier > 0:
                nc.gpsimd.wait_ge(pool_carried, earlier)
            nc.gpsimd.tensor_tensor(carried[:, 0:1], minus_half[:, 0:1], minus_half[:, 0:1], ALU.mult
                                    ).then_inc(pool_carried, 1)

        block = stack.enter_context(nc.Block())

        @block.sync
        def _(sp):
            def load(t):
                if not t.exists():
                    return
                src = x_t[bass.ds(t.n, 1)].rearrange("a p n -> (a p) n")
                src_c = c_t[bass.ds(t.n, 1)].rearrange("a p n -> (a p) n")
                if t.at_least(2):
                    sp.wait_ge(x2_sb, t.n - 1)
                    sp.wait_ge(ctxT_ps, t.n - 1)
                sp.dma_start(x_sb[t.par][:], src).then_inc(x_in[t.par], 16)
                sp.dma_start(c_sb[t.par][:], src_c).then_inc(c_in[t.par], 16)

            def store(t):
                if not t.exists():
                    return
                sp.wait_ge(out_ready, t.n + 1)
                sp.dma_start(out_t[bass.ds(t.n, 1)].rearrange("a p n -> (a p) n"),
                             out_sb[t.par][:]).then_inc(stored[t.par], 16)

            sp.dma_start(x_sb[0][:], x_t[0]).then_inc(x_in[0], 16)
            sp.dma_start(cst[:], consts).then_inc(consts_in, 16)
            sp.dma_start(c_sb[0][:], c_t[0]).then_inc(c_in[0], 16)
            for dst, src in ((w_k, wk), (vec, vecs), (w_q, wq), (w_v, wv), (w_c, wc)):
                sp.dma_start(dst[:], src).then_inc(attention_in, 16)
            sp.dma_start(bias_in[:], bias_rows.rearrange("p (m n) -> p m n", m=2)).then_inc(attention_in, 16)
            sp.dma_start(x_sb[1][:], x_t[1]).then_inc(x_in[1], 16)
            sp.dma_start(c_sb[1][:], c_t[1]).then_inc(c_in[1], 16)
            sp.dma_start(w_r[:], router).then_inc(ffn_in, 16)
            sp.dma_start(w_s1[:], sw1).then_inc(ffn_in, 16)
            sp.dma_start(w_s2[:], sw2.rearrange("(c p) o -> p c o", p=P)).then_inc(ffn_in, 16)
            sp.dma_start(tab[:], tables).then_inc(ffn_in, 16)
            sp.wait_ge(setup, 1)
            sp.dma_start(rows_dram[PAD_ROW:PAD_ROW + TILE].rearrange("(p s) n -> p (s n)", s=SUB),
                         pad[:]).then_inc(pads_in, 16)
            sp.dma_start(out[TOKENS:OUT_ROWS].rearrange("(p s) n -> p s n", s=SUB),
                         pad[:, :, 0:D]).then_inc(dummies_in, 16)

            def step(t):
                if t.at_least(2) and not (t.static and t.n == TILES + 1):
                    store(t.later(-2))
                if t.exists():
                    load(t.later(2))

            pipeline(sp, step)

            def load_weights(t):
                if not t.exists():
                    return
                e = sp.value_load(expert_of[0:1, bass.ds(t.n, 1)], min_val=0, max_val=E - 1)
                if t.at_least(DEEP):
                    sp.wait_ge(w2_lo, t.n - DEEP + 1)
                    sp.wait_ge(w1_lo, t.n - DEEP + 1)
                sp.dma_start(w1b[t.par][:], ew1[bass.ds(e, 1)].rearrange("a p n -> (a p) n")
                             ).then_inc(w_in[t.par], 16)
                sp.dma_start(w2b[t.par][:], ew2[bass.ds(e, 1)].rearrange("a (c p) n -> p (a c) n", p=P)
                             ).then_inc(w_in[t.par], 16)

            def load_extra(t):
                if not t.exists():
                    return
                e = sp.value_load(expert_of[0:1, bass.ds(t.n, 1)], min_val=0, max_val=E - 1)
                if t.at_least(DEEP):
                    sp.wait_ge(byT_sb, t.n - DEEP + 1)
                sp.dma_start(exb[t.par][:], extra[bass.ds(e, 1)].rearrange("a p n -> (a p) n")
                             ).then_inc(exb_in[t.par], 16)

            def load_rows(t):
                if not t.exists():
                    return
                row = sp.value_load(row_of[0:1, bass.ds(t.n, 1)], min_val=0, max_val=PAD_ROW)
                if t.static and t.n < DEEP:
                    k = t.n
                    pads = sp.value_load(need_pads[0:1, k:k + 1], min_val=16, max_val=16 * (E + 1))
                    last_rows = sp.value_load(need_rows[0:1, k:k + 1], min_val=SCAT_ALL - 16 * SCATTERS,
                                              max_val=SCAT_ALL)
                    sp.wait_ge(pads_in, pads)
                    sp.wait_ge(scattered[0], SCAT_ALL)
                    sp.wait_ge(scattered[1], last_rows)
                if t.at_least(DEEP):
                    sp.wait_ge(w_sb, t.n - DEEP + 1)
                sp.dma_start(xb[t.par][:], rows_dram[bass.ds(row, TILE)].rearrange("(p s) n -> p (s n)", s=SUB)
                             ).then_inc(xb_in[t.par], 16)

            sp.wait_ge(table_done, 1)
            load_rows(XFIRST)
            load_weights(XFIRST)
            load_extra(XFIRST)
            load_weights(XFIRST.later(1))
            load_rows(XFIRST.later(1))
            load_rows(XFIRST.later(2))
            load_weights(XFIRST.later(2))
            store(Tile(0, TILES - 1))
            sp.wait_ge(pads_in, 16 * (E + 1))
            for k in range(2):
                sp.wait_ge(scattered[k], SCAT_ALL)

            def step(t):
                load_weights(t.later(DEEP))
                load_extra(t.later(1))
                load_rows(t.later(DEEP))

            experts(sp, step, 0)
            sp.wait_ge(added, ADDED * XTILES)

        @block.tensor
        def _(pe):
            mm, tr = nc.tensor.matmul, nc.tensor.transpose
            pe.wait_ge(consts_in, 16)

            def turn(dst, src):
                for s in range(SUB):
                    last = tr(dst[:, s * P:(s + 1) * P], src(s), ident)
                return last

            def product(dst, stationary, moving, start=True, stop=True):
                mm(dst, stationary(HI), moving(HI), start=start, stop=False)
                mm(dst, stationary(HI), moving(LO), start=False, stop=False)
                return mm(dst, stationary(LO), moving(HI), start=False, stop=stop)

            PROJ_BIAS, SHARED_BIAS = 0, 1

            def add_bias(dst, which):
                mm(dst, ones_r[:], bias_parts[:, which, :], start=True, stop=False, skip_group_check=True)

            def turn_context(t):
                if t.exists():
                    pe.wait_ge(c_in[t.par], 16 * (t.half + 1))
                    turn(ps_ctxT, lambda s: c_sb[t.par][:, s, :]).then_inc(ctxT_ps, 1)

            def step(t):
                u, v = t.later(-1), t.later(-2)
                has_u, has_v = u.exists(), v.exists()

                def hidden(c):
                    product(ps_h[c][:], lambda part: ws1[part][:, c * P:(c + 1) * P],
                            lambda part: ns[v.par][part][:]).then_inc(h_ps, 1)

                def second(c):
                    pe.wait_ge(h_sb, v.n * HC + c + 1)
                    for s in range(SUB):
                        last = mm(ps_y[:, s * D:(s + 1) * D], hT[:, c, s * P:(s + 1) * P], w_s2[:, c, :],
                                  start=False, stop=(c == HC - 1), skip_group_check=True)
                    if c == HC - 1:
                        last.then_inc(y_ps, 1)

                def first_result():
                    if t.exists():
                        pe.wait_ge(q_parts, t.n + 1)
                    else:
                        pe.wait_ge(out_ready, v.n)
                    add_bias(ps_y[:], SHARED_BIAS)
                    second(0)

                if t.exists():
                    pe.wait_ge(xn_sb, t.n + 1)
                    if t.at_least(3):
                        pe.wait_ge(h_sb, (t.n - 2) * HC)
                    turn(ps_xT, lambda s: xn[:, s, :]).then_inc(xT_ps, 1)
                if not t.exists() and not has_u and has_v:
                    pe.wait_ge(route, v.n * ROUTE_STEPS + CHOSEN)
                    pe.wait_ge(seen_sb, v.n)
                    pe.wait_ge(x2_sb, TILES)
                    mm(ps_count[:, E:2 * E], ones_b[:], seen[:], start=True, stop=True, skip_group_check=True)
                    mm(ps_count[:, 0:E], ones_b[:], seen[:], start=True, stop=False, skip_group_check=True)
                    for s in range(SUB):
                        last = mm(ps_count[:, 0:E], ones_b[:], chosen[:, s, :], start=False, stop=(s == SUB - 1),
                                  skip_group_check=True)
                    last.then_inc(count_ps, 1)
                if has_v:
                    pe.wait_ge(route, v.n * ROUTE_STEPS + CHOSEN)
                    every = chosen[:].rearrange("p s e -> p (s e)")
                    by_sub = ps_rank.rearrange("p (s e) -> p s e", s=SUB)
                    mm(ps_rank, before_b[:], every, start=True, stop=False)
                    for s in range(SUB - 1):
                        mm(by_sub[:, s + 1:SUB, :], ones_b[:],
                           chosen[:, s:s + 1, :].to_broadcast([P, SUB - 1 - s, E]),
                           start=False, stop=False, skip_group_check=True)
                    if v.at_least(1):
                        pe.wait_ge(seen_sb, v.n)
                    mm(by_sub, ones_b[:], seen[:].unsqueeze(1).to_broadcast([P, SUB, E]),
                       start=False, stop=True).then_inc(rank_ps, 1)
                if t.exists():
                    if t.static and t.n == 0:
                        pe.wait_ge(attention_in, ATTENTION_IN)
                    pe.wait_ge(ctxT_sb, t.n + 1)
                    mm(ps_k[:], w_k[:], ctxT[:], start=True, stop=True).then_inc(k_ps, 1)
                    pe.wait_ge(xnT_sb, t.n + 1)
                    if t.at_least(3):
                        pe.wait_ge(out_ready, t.n - 2)
                    mm(ps_q[:], w_q[:], xnT[:], start=True, stop=True).then_inc(q_ps, 1)
                    mm(ps_v[:], w_v[:], ctxT[:], start=True, stop=True).then_inc(v_ps, 1)
                if has_v:
                    pe.wait_ge(n_lo, v.n + 1)
                    pe.wait_ge(n_hi, v.n + 1)
                    if v.static and v.n == 0:
                        pe.wait_ge(ws1_lo, 1)
                    hidden(0)
                if t.exists():
                    pe.wait_ge(kT_sb, t.n + 1)
                    if t.at_least(1):
                        pe.wait_ge(x2_sb, t.n)
                    mm(ps_csum[:], heads, kT[:], start=True, stop=True).then_inc(csum_ps, 1)
                if has_v:
                    if t.exists():
                        pe.wait_ge(xnT_sb, t.n + 1)
                    hidden(1)
                    hidden(2)
                    if t.exists():
                        pe.wait_ge(k_parts, t.n + 1)
                    hidden(3)
                    if not t.exists():
                        first_result()
                    pe.wait_ge(h_sb, v.n * HC + 1)
                if has_u:
                    pe.wait_ge(rows_sb, u.n + 1)
                    turn(ps_nT, lambda s: rows[u.par][:, s, 0:D]).then_inc(nT_ps, 1)
                if has_v:
                    if t.exists():
                        first_result()
                    else:
                        second(1)
                if has_u:
                    pe.wait_ge(nT_sb, u.n + 1)
                    if u.at_least(1):
                        pe.wait_ge(place_sb, u.n)
                    for s in range(SUB):
                        last = mm(ps_logit[:, s * E:(s + 1) * E], nT[:, s * P:(s + 1) * P], w_r[:],
                                  start=True, stop=True)
                    last.then_inc(logit_ps, 1)
                if has_v:
                    if t.exists():
                        second(1)
                    second(2)
                    second(3)
                if t.exists():
                    pe.wait_ge(ctxT_sb, t.n + 1)
                turn_context(t.later(1))
                if t.exists():
                    pe.wait_ge(attn_sb, t.n + 1)
                    if t.static and t.n == 0:
                        pe.wait_ge(bias_sb, 1)
                        pe.wait_ge(ffn_in, FFN_IN)
                    add_bias(ps_proj[:], PROJ_BIAS)
                    for s in range(SUB):
                        last = mm(ps_proj[:, s * D:(s + 1) * D], attnT[:, s * P:(s + 1) * P], w_c[:],
                                  start=False, stop=True, skip_group_check=True)
                    last.then_inc(proj_ps, 1)

            turn_context(FIRST)
            pipeline(pe, step)

            def turn_in(t):
                pe.wait_ge(xb_in[t.par], 16 * (t.half + 1))
                if t.at_least(1):
                    pe.wait_ge(xs_lo, t.n)
                turn(pb_xT, lambda s: xb[t.par][:, s, 0:D]).then_inc(bxT_ps, 1)

            def expert_step(t):
                v, w = t.later(-1), t.later(-2)

                def hidden(c):
                    if t.at_least(1):
                        pe.wait_ge(h_hi, (t.n - 1) * HC + c + 1)
                    product(pb_h[c][:], lambda part: w1s[t.par][part][:, c * P:(c + 1) * P],
                            lambda part: xs[t.par][part][:]).then_inc(bh_ps, 1)

                if t.exists():
                    pe.wait_ge(xs_lo, t.n + 1)
                    pe.wait_ge(w1_lo, t.n + 1)
                    hidden(0)
                if t.later(1).exists():
                    turn_in(t.later(1))
                if w.exists():
                    pe.wait_ge(byT_sb, w.n + 1)
                    if w.at_least(1):
                        pe.wait_ge(by_sb, w.n)
                    turn(pb_y, lambda s: yT[:, s * P:(s + 1) * P]).then_inc(by_ps, 1)
                if t.exists():
                    for c in range(1, HC):
                        hidden(c)
                if v.exists():
                    pe.wait_ge(w2_lo, v.n + 1)
                    for c in range(HC):
                        pe.wait_ge(h_lo, v.n * HC + c + 1)
                        last = product(pb_yT[:], lambda part: w2s[v.par][part][:, c, :],
                                       lambda part: hs[v.par][part][:, c, :], c == 0, c == HC - 1)
                    last.then_inc(byT_ps, 1)

            pe.wait_ge(out_ready, TILES)
            turn_in(XFIRST)
            experts(pe, expert_step, 2)

        @block.scalar
        def _(act):
            fn = nc.scalar.activation

            def feature(col):
                return vec[:, col:col + 1]

            def normalise(which, dst, src):
                for s in range(SUB):
                    last = fn(dst(s), src(s), ACT.Identity, bias=shift[which][:, s:s + 1],
                              scale=rstd[which][:, s:s + 1])
                return last

            def norm_x(t):
                if t.exists():
                    act.wait_ge(shift_sb[0], t.n + 1)
                    normalise(0, lambda s: xn[:, s, :], lambda s: x_sb[t.par][:, s, :]).then_inc(xn_sb, 1)

            def copy_context(t):
                if t.exists():
                    act.wait_ge(ctxT_ps, t.n + 1)
                    fn(ctxT[:], ps_ctxT[:], ACT.Copy).then_inc(ctxT_sb, 1)

            norm_x(FIRST)
            copy_context(FIRST)
            act.wait_ge(attention_in, ATTENTION_IN)

            def step(t):
                u, v = t.later(-1), t.later(-2)
                has_u, has_v = u.exists(), v.exists()

                def hidden(c):
                    act.wait_ge(h_ps, v.n * HC + c + 1)
                    fn(hT[:, c, :], ps_h[c][:], ACT.Relu, bias=feature(V_SB1 + c)).then_inc(h_sb, 1)

                if t.exists():
                    act.wait_ge(xT_ps, t.n + 1)
                    fn(xnT[:], ps_xT[:], ACT.Copy).then_inc(xnT_sb, 1)
                    act.wait_ge(k_ps, t.n + 1)
                    fn(k_exp[:], ps_k[:], ACT.Exp, bias=feature(V_BK))
                    fn(k_lin[:], ps_k[:], ACT.Relu, bias=feature(V_BK)).then_inc(k_parts, 1)
                if t.exists():
                    act.wait_ge(q_ps, t.n + 1)
                    fn(q_exp[:], ps_q[:], ACT.Exp, bias=feature(V_BQ))
                    fn(q_lin[:], ps_q[:], ACT.Relu, bias=feature(V_BQ)).then_inc(q_parts, 1)
                if has_v:
                    if v.at_least(1):
                        act.wait_ge(y_ps, v.n)
                    hidden(0)
                if has_u:
                    act.wait_ge(shift_sb[1], u.n + 1)
                    if u.at_least(2):
                        act.wait_ge(scattered[u.par], 16 * SCATTERS * u.half)
                    normalise(1, lambda s: rows[u.par][:, s, 0:D], lambda s: x2[u.par][:, s, :]
                              ).then_inc(rows_sb, 1)
                if has_v:
                    hidden(1)
                    hidden(2)
                if has_u:
                    act.wait_ge(nT_ps, u.n + 1)
                    if u.at_least(1):
                        act.wait_ge(n_lo, u.n)
                        act.wait_ge(logit_ps, u.n)
                    fn(nT[:], ps_nT[:], ACT.Identity, scale=feature(V_NW)).then_inc(nT_sb, 1)
                    fn(ns[u.par][HI][:], ps_nT[:], ACT.Identity, scale=feature(V_NW)).then_inc(n_hi, 1)
                if has_v:
                    hidden(3)
                if has_u:
                    act.wait_ge(key_sb, u.n + 1)
                    fn(e_neg[:], key[:], ACT.Exp, scale=-1.0).then_inc(e_sb, 1)
                norm_x(t.later(1))
                copy_context(t.later(1))

            pipeline(act, step)

            act.wait_ge(pad_at_sb, 1)
            for e in range(E):
                at = act.value_load(pad_at[0:1, e:e + 1], min_val=e * REGION, max_val=e * REGION + TOKENS)
                act.dma_start(rows_dram[bass.ds(at, TILE)].rearrange("(p s) n -> p (s n)", s=SUB),
                              pad[:]).then_inc(pads_in, 16)

            def rows_high(t):
                if t.exists():
                    act.wait_ge(bxT_ps, t.n + 1)
                    fn(xs[t.par][HI][:], pb_xT[:], ACT.Identity, scale=feature(V_NW)).then_inc(xs_hi, 1)

            def expert_step(t):
                w = t.later(-2)

                def hidden(c):
                    bias = exb[t.par][:, COL_B1 + c:COL_B1 + c + 1]
                    act.wait_ge(bh_ps, t.n * HC + c + 1)
                    if t.at_least(1):
                        act.wait_ge(h_lo, (t.n - 1) * HC + c + 1)
                    fn(hT[:, c, :], pb_h[c][:], ACT.Relu, bias=bias)
                    fn(hs[t.par][HI][:, c, :], pb_h[c][:], ACT.Relu, bias=bias).then_inc(h_hi, 1)

                if w.exists():
                    act.wait_ge(byT_ps, w.n + 1)
                    fn(yT[:], pb_yT[:], ACT.Identity, bias=exb[w.par][:, COL_B2:COL_B2 + 1]).then_inc(byT_sb, 1)
                rows_high(t.later(1))
                if t.exists():
                    act.wait_ge(exb_in[t.par], 16 * (t.half + 1))
                    for c in range(HC):
                        hidden(c)

            rows_high(XFIRST)
            experts(act, expert_step, 2)

        @block.gpsimd
        def _(pool):
            def scatter(t, which, subs=range(SUB)):
                for s in subs:
                    pool.indirect_dma_start(
                        rows_dram, bass.IndirectOffsetOnAxis(ap=slot[t.par][:, which, s:s + 1], axis=0),
                        rows[t.par][:, s, :], None).then_inc(scattered[t.par], 16)

            def raise_power(which, t):
                pool.wait_ge(spread_sb[which], t.n + 1)
                nc.gpsimd.tensor_tensor(rstd[which][:], spread[which][:], minus_half[:], ALU.pow
                                        ).then_inc(power[which], 1)
                pool.wait_ge(power[which], t.n + 1)
                nc.gpsimd.tensor_tensor(shift[which][:], neg_mean[which][:], rstd[which][:], ALU.mult
                                        ).then_inc(shift_sb[which], 1)

            raise_power(0, FIRST)

            def step(t):
                u, v = t.later(-1), t.later(-2)
                has_v = v.exists()
                if u.exists():
                    raise_power(1, u)
                if has_v:
                    pool.wait_ge(slot_sb, v.n + 1)
                    pool.wait_ge(routed, v.n + 1)
                    pool.wait_ge(rows_sb, v.n + 1)
                    carry_wait_pool(v.n)
                    scatter(v, 0, range(0, 2))
                if t.exists():
                    pool.wait_ge(qT_sb, t.n + 1)
                    pool.wait_ge(kT_sb, t.n + 1)
                    nc.gpsimd.tensor_tensor(qk[:], qT[:], kT[:], ALU.mult).then_inc(qk_sb, 1)
                if t.later(1).exists():
                    raise_power(0, t.later(1))
                if has_v:
                    scatter(v, 0, range(2, SUB))
                    scatter(v, 1)

            pipeline(pool, step)
            def second_low(t):
                if t.exists():
                    pool.wait_ge(w2_hi, t.n + 1)
                    nc.gpsimd.tensor_tensor(w2s[t.par][LO][:], w2b[t.par][:], w2s[t.par][HI][:].bitcast(F32),
                                            ALU.subtract).then_inc(w2_lo, 1)

            def expert_step(t):
                w = t.later(-2)
                if w.exists():
                    pool.wait_ge(by_sb, w.n + 1)
                    if w.at_least(1):
                        pool.wait_ge(added, ADDED * w.n)
                    carry_wait_pool(TILES + w.n)
                    for s in range(SUB):
                        pool.indirect_dma_start(
                            out, bass.IndirectOffsetOnAxis(ap=tok[w.par][:, s:s + 1], axis=0),
                            yb[w.par][:, s, :], None, compute_op=ALU.add).then_inc(added, 16)
                second_low(t.later(1))

            second_low(XFIRST)
            for k in range(2):
                pool.wait_ge(stored[k], 16 * TILES // 2)
            pool.wait_ge(dummies_in, 16)
            experts(pool, expert_step, 2)

        @block.vector
        def _(dve):
            v_ = nc.vector

            def feature(col):
                return vec[:, col:col + 1]

            class Steps:

                def __init__(self, sem, n, per):
                    self.sem, self.start, self.k = sem, n * per, 0

                def then(self, ins):
                    ins.then_inc(self.sem, 1)
                    self.k += 1

                def wait(self):
                    dve.wait_ge(self.sem, self.start + self.k)

            def sums(which, t, src, subs=range(SUB)):
                for s in subs:
                    last = v_.bn_stats(st[which][:, s, :], src[:, s, :])
                if s == SUB - 1:
                    last.then_inc(stat[which], 1)

            def moments(which, t):
                dve.wait_ge(stat[which], 2 * t.n + 1)
                carry_wait_dve()
                for s in range(SUB):
                    last = v_.bn_aggr(mv[which][:, s, :], st[which][:, s, :])
                last.then_inc(stat[which], 1)

            def spreads(which, t):
                dve.wait_ge(stat[which], 2 * t.n + 2)
                if t.at_least(1):
                    dve.wait_ge(shift_sb[which], t.n)
                v_.tensor_scalar(neg_mean[which][:], mv[which][:, :, 0], -1.0, None, ALU.mult)
                if which == 0:
                    scale, eps = 1.0, LN_EPS
                else:
                    scale, eps = 1.0 + RMS_EPS, LN_EPS * RMS_EPS
                v_.tensor_scalar(spread[which][:], mv[which][:, :, 1], scale, eps, ALU.mult, ALU.add
                                 ).then_inc(spread_sb[which], 1)

            v_.memset(minus_half[:], -0.5)
            dve.wait_ge(x_in[0], 16)
            sums(0, FIRST, x_sb[0])
            moments(0, FIRST)
            spreads(0, FIRST)
            dve.wait_ge(consts_in, 16)
            v_.memset(seen[:], 0.0)
            v_.memset(score[:, :, E:E + 1], COMB_EPS)
            v_.tensor_copy(before_b[:], cst[:, CM_BEFORE:CM_BEFORE + P])
            v_.tensor_copy(ones_b[:], cst[:, CM_ONES:CM_ONES + P])
            v_.memset(pad[:, :, 0:COL_ID], 0.0)
            v_.memset(pad[:, :, COL_ID + 1:ROW], 0.0)
            for k in range(2):
                v_.memset(rows[k][:, :, COL_ID + 1:ROW], 0.0)
            v_.tensor_scalar(rows[1][:, :, COL_ID], id0, float(-TILE), None, ALU.add)
            v_.tensor_scalar(pad[:, :, COL_ID], id0, float(TOKENS), None, ALU.add).then_inc(setup, 1)
            dve.wait_ge(setup, 1)
            dve.wait_ge(attention_in, ATTENTION_IN)
            v_.tensor_copy(ones_r[:], cst[0:2, CM_ONES:CM_ONES + P])
            v_.tensor_scalar(bias_share[:], bias_in[:], cst[0:2, CS_WHOLE:CS_WHOLE + 1], None, ALU.mult)
            v_.tensor_copy(bias_hi[:], bias_in[:]).then_inc(bias_steps, 1)
            dve.wait_ge(bias_steps, 1)
            v_.scalar_tensor_tensor(bias_parts[:], bias_hi[:].bitcast(F32), cst[0:2, CS_SIGN:CS_SIGN + 1],
                                    bias_share[:], ALU.mult, ALU.add).then_inc(bias_sb, 1)

            def done(ins):
                ins.then_inc(route, 1)

            def wait(u, k):
                dve.wait_ge(route, u.n * ROUTE_STEPS + k)

            def order_keys(u):
                dve.wait_ge(key_sb, u.n + 1)
                carry_wait_dve()
                for s in range(SUB):
                    last = v_.max(sorted_key[:, s, :], key[:, s, :])
                done(last)

            def choose(u):
                wait(u, 1)
                carry_wait_dve()
                for s in range(SUB):
                    last = v_.max_index(sorted_at[:, s, :], sorted_key[:, s, :], key[:, s, :])
                done(last)
                dve.wait_ge(e_sb, u.n + 1)
                done(v_.tensor_scalar(den[:], e_neg[:], 1.0, None, ALU.add))
                wait(u, 3)
                done(v_.reciprocal(prob[:], den[:]))
                four = [P, SUB, TOPK, E]
                done(v_.tensor_tensor(hot[:].rearrange("p i s e -> p s i e"),
                                      sorted_at[:, :, 0:TOPK].unsqueeze(3).to_broadcast(four),
                                      expert_no.unsqueeze(1).unsqueeze(1).to_broadcast(four), ALU.is_equal))
                dve.wait_ge(n_hi, u.n + 1)
                v_.tensor_tensor(ns[u.par][LO][:], nT[:], ns[u.par][HI][:].bitcast(F32), ALU.subtract
                                 ).then_inc(n_lo, 1)
                wait(u, 5)
                if u.at_least(1):
                    dve.wait_ge(rank_ps, u.n)
                done(v_.tensor_tensor(chosen[:], hot[:, 0], hot[:, 1], ALU.add))

            def score_chosen(v):
                wait(v, 6)
                done(v_.tensor_tensor(score[:, :, 0:E], prob[:], chosen[:], ALU.mult))

            def add_scores(v):
                wait(v, 7)
                done(v_.tensor_reduce(total[:], score[:], AX, ALU.add))

            def invert_sum(v):
                wait(v, 8)
                done(v_.reciprocal(inv_total[:], total[:]))

            def finish_rows(v):
                wait(v, 9)
                if v.at_least(2):
                    dve.wait_ge(scattered[v.par], 16 * SCATTERS * v.half)
                v_.tensor_tensor(rows[v.par][:, :, COL_W:COL_W + E], score[:, :, 0:E],
                                 inv_total[:].unsqueeze(2).to_broadcast([P, SUB, E]), ALU.mult)
                v_.tensor_scalar(rows[v.par][:, :, COL_ID], rows[1 - v.par][:, :, COL_ID], float(TILE), None,
                                 ALU.add).then_inc(routed, 1)

            def split_shared():
                dve.wait_ge(ffn_in, FFN_IN)
                v_.tensor_copy(ws1[HI][:], w_s1[:]).then_inc(ws1_hi, 1)
                dve.wait_ge(ws1_hi, 1)
                v_.tensor_tensor(ws1[LO][:], w_s1[:], ws1[HI][:].bitcast(F32), ALU.subtract).then_inc(ws1_lo, 1)

            def step(t):
                n, u, v = t.later(1), t.later(-1), t.later(-2)
                has_t, has_n, has_u, has_v = t.exists(), n.exists(), u.exists(), v.exists()

                if has_u:
                    dve.wait_ge(x2_sb, u.n + 1)
                    sums(1, u, x2[u.par])
                if has_v:
                    score_chosen(v)
                if has_u:
                    moments(1, u)
                if has_v:
                    add_scores(v)
                if has_u:
                    spreads(1, u)
                if has_v:
                    invert_sum(v)
                if has_t:
                    dve.wait_ge(k_parts, t.n + 1)
                    v_.scalar_tensor_tensor(kT[:], k_exp[:], 1.0, k_lin[:], ALU.min, ALU.add
                                            ).then_inc(kT_sb, 1)
                if has_v:
                    finish_rows(v)
                if has_v:
                    dve.wait_ge(rank_ps, v.n + 1)
                    dve.wait_ge(routed, v.n + 1)
                    v_.tensor_tensor(place[:], ps_rank.rearrange("p (s e) -> p s e", s=SUB), base, ALU.add
                                     ).then_inc(place_sb, 1)
                    v_.tensor_reduce(tile_count[:], chosen[:].rearrange("p s e -> p e s"), AX, ALU.add
                                     ).then_inc(counted, 1)
                    dve.wait_ge(place_sb, v.n + 1)
                    v_.tensor_tensor(placed[:], hot[:], place[:].unsqueeze(1).to_broadcast([P, TOPK, SUB, E]),
                                     ALU.mult).then_inc(placed_sb, 1)
                    dve.wait_ge(counted, v.n + 1)
                    v_.tensor_tensor(seen[:], seen[:], tile_count[:], ALU.add).then_inc(seen_sb, 1)
                if has_n:
                    dve.wait_ge(x_in[n.par], 16 * (n.half + 1))
                    sums(0, n, x_sb[n.par], (0,))
                if has_v:
                    dve.wait_ge(placed_sb, v.n + 1)
                    v_.tensor_reduce(slot_f[:], placed[:], AX, ALU.add).then_inc(slot_f_sb, 1)
                if has_n:
                    sums(0, n, x_sb[n.par], (1, 2, 3))
                if has_v:
                    dve.wait_ge(slot_f_sb, v.n + 1)
                    if v.at_least(2):
                        dve.wait_ge(scattered[v.par], 16 * SCATTERS * v.half)
                    v_.tensor_copy(slot[v.par][:], slot_f[:]).then_inc(slot_sb, 1)
                    if not has_t and not has_u:
                        make_table()
                if has_n:
                    moments(0, n)
                if has_t:
                    dve.wait_ge(q_parts, t.n + 1)
                    v_.scalar_tensor_tensor(qT[:], q_exp[:], 1.0, q_lin[:], ALU.min, ALU.add
                                            ).then_inc(qT_sb, 1)
                if has_n:
                    spreads(0, n)
                if has_t:
                    dve.wait_ge(csum_ps, t.n + 1)
                    v_.reciprocal(k_inv[:], ps_csum[:]).then_inc(inv_sb, 1)
                if has_u:
                    dve.wait_ge(logit_ps, u.n + 1)
                    v_.tensor_scalar(key[:], ps_logit.rearrange("p (s e) -> p s e", s=SUB), SIG_ONE, SIG_ZERO,
                                     ALU.min, ALU.max).then_inc(key_sb, 1)
                if has_t:
                    dve.wait_ge(inv_sb, t.n + 1)
                    dve.wait_ge(qk_sb, t.n + 1)
                    v_.tensor_tensor(qkn[:], qk[:], k_inv[:], ALU.mult).then_inc(qkn_sb, 1)
                if has_u:
                    order_keys(u)
                if has_t:
                    dve.wait_ge(qkn_sb, t.n + 1)
                    dve.wait_ge(v_ps, t.n + 1)
                    v_.scalar_tensor_tensor(attnT[:], ps_v[:], feature(V_BV), qkn[:], ALU.add, ALU.mult
                                            ).then_inc(attn_sb, 1)
                    if t.static and t.n == 0:
                        split_shared()
                if has_u:
                    choose(u)
                if has_v:
                    dve.wait_ge(y_ps, v.n + 1)
                    if v.at_least(2):
                        dve.wait_ge(stored[v.par], 16 * v.half)
                    v_.tensor_tensor(out_sb[v.par][:].rearrange("p s d -> p (s d)"), ps_y[:],
                                     x2[v.par][:].rearrange("p s d -> p (s d)"), ALU.add).then_inc(out_ready, 1)
                if has_t:
                    dve.wait_ge(proj_ps, t.n + 1)
                    if has_v:
                        dve.wait_ge(out_ready, v.n + 1)
                    v_.tensor_tensor(x2[t.par][:].rearrange("p s d -> p (s d)"), ps_proj[:],
                                     x_sb[t.par][:].rearrange("p s d -> p (s d)"), ALU.add).then_inc(x2_sb, 1)

            def make_table():
                c = Steps(table, 0, 0)

                def do(ins):
                    c.then(ins)
                    c.wait()

                step_t = tab[:, TB_STEP:TB_UPTO].rearrange("a (e m) -> a e m", e=E)
                upto_t = tab[:, TB_UPTO:TB_TILE].rearrange("a (e m) -> a e m", e=E)
                tile_t, reg_t = tab[:, TB_TILE:TB_REG], tab[:, TB_REG:TB_REG + E]
                dve.wait_ge(ffn_in, FFN_IN)
                dve.wait_ge(count_ps, 1)
                count, count_before = cnt[:, 0:E], cnt[:, E:2 * E]
                do(v_.tensor_copy(cnt[:], ps_count[0:1, :]))
                v_.tensor_tensor(pad_at[:], count, reg_t, ALU.add).then_inc(pad_at_sb, 1)
                v_.tensor_tensor(tl_whole[:], count_before.unsqueeze(2).to_broadcast([1, E, TILES]), step_t,
                                 ALU.is_ge)
                do(v_.tensor_tensor(tl_a[:], count.unsqueeze(2).to_broadcast([1, E, TILES]), step_t, ALU.is_gt))
                v_.tensor_reduce(tl_whole_n[:], tl_whole[:], AX, ALU.add)
                do(v_.tensor_reduce(tl_n[:], tl_a[:], AX, ALU.add))
                do(v_.tensor_tensor(tl_b[:], tl_n[:].unsqueeze(1).to_broadcast([1, E, E]), upto_t, ALU.mult))
                do(v_.tensor_reduce(tl_end[:], tl_b[:], AX, ALU.add))
                v_.tensor_tensor(tl_start[:], tl_end[:], tl_n[:], ALU.subtract)
                many, few = [1, XTILES, E], [1, DEEP, E]
                do(v_.tensor_tensor(tl_past[:], tile_t.unsqueeze(2).to_broadcast(many),
                                    tl_end[:].unsqueeze(1).to_broadcast(many), ALU.is_ge))
                v_.scalar_tensor_tensor(tl_stop[:], tl_whole_n[:], -1.0, tl_start[:], ALU.add, ALU.add)
                do(v_.tensor_reduce(tl_e[:], tl_past[:], AX, ALU.add))
                few_t = tile_t[:, 0:DEEP].unsqueeze(2).to_broadcast(few)
                v_.tensor_tensor(tl_from[:], few_t, tl_start[:].unsqueeze(1).to_broadcast(few), ALU.is_ge)
                v_.tensor_tensor(tl_to[:], few_t, tl_stop[:].unsqueeze(1).to_broadcast(few), ALU.is_lt)
                do(v_.tensor_tensor(tl_used[:], tl_past[:], tl_n[:].unsqueeze(1).to_broadcast(many), ALU.mult))
                v_.tensor_tensor(tl_in[:], tl_from[:], tl_to[:], ALU.mult)
                do(v_.tensor_reduce(tl_first[:], tl_used[:], AX, ALU.add))
                v_.tensor_reduce(tl_early[:], tl_in[:], AX, ALU.add)
                do(v_.tensor_tensor(tl_k[:], tile_t, tl_first[:], ALU.subtract))
                v_.tensor_scalar(need_pads[:], tl_early[:], -float(16 * E), float(16 * (E + 1)), ALU.mult, ALU.add)
                v_.tensor_scalar(need_rows[:], tl_early[:], -float(16 * SCATTERS), float(SCAT_ALL), ALU.mult,
                                 ALU.add)
                do(v_.tensor_scalar(tl_base[:], tl_e[:], float(REGION), None, ALU.mult))
                do(v_.scalar_tensor_tensor(tl_row[:], tl_k[:], float(TILE), tl_base[:], ALU.mult, ALU.add))
                do(v_.tensor_scalar(expert_of[:], tl_e[:], float(E - 1), None, ALU.min))
                v_.tensor_scalar(row_of[:], tl_row[:], float(PAD_ROW), None, ALU.min).then_inc(table_done, 1)

            pipeline(dve, step)

            def split_weights(t):
                if not t.exists():
                    return
                dve.wait_ge(w_in[t.par], 32 * (t.half + 1))
                if t.at_least(DEEP):
                    dve.wait_ge(byT_ps, t.n - DEEP + 1)
                v_.tensor_copy(w1s[t.par][HI][:], w1b[t.par][:]).then_inc(w1_hi, 1)
                v_.tensor_copy(w2s[t.par][HI][:], w2b[t.par][:]).then_inc(w2_hi, 1)
                dve.wait_ge(w1_hi, t.n + 1)
                v_.tensor_tensor(w1s[t.par][LO][:], w1b[t.par][:], w1s[t.par][HI][:].bitcast(F32), ALU.subtract
                                 ).then_inc(w1_lo, 1)

            def rows_low(t):
                if t.exists():
                    dve.wait_ge(xs_hi, t.n + 1)
                    v_.scalar_tensor_tensor(xs[t.par][LO][:], pb_xT[:], feature(V_NW), xs[t.par][HI][:].bitcast(F32),
                                            ALU.mult, ALU.subtract).then_inc(xs_lo, 1)

            def expert_step(t):
                w = t.later(-2)

                def hidden_low(c):
                    dve.wait_ge(h_hi, t.n * HC + c + 1)
                    v_.tensor_tensor(hs[t.par][LO][:, c, :], hT[:, c, :], hs[t.par][HI][:, c, :].bitcast(F32),
                                     ALU.subtract).then_inc(h_lo, 1)

                if w.exists():
                    dve.wait_ge(by_ps, w.n + 1)
                    if w.at_least(DEEP):
                        dve.wait_ge(added, ADDED * (w.n - DEEP + 1))
                    v_.tensor_tensor(yb[w.par], pb_y.rearrange("p (s d) -> p s d", s=SUB),
                                     w_row[w.par][:].unsqueeze(2).to_broadcast([P, SUB, D]), ALU.mult
                                     ).then_inc(by_sb, 1)
                split_weights(t.later(1))
                rows_low(t.later(1))
                if t.exists():
                    for c in range(HC):
                        hidden_low(c)
                    dve.wait_ge(exb_in[t.par], 16 * (t.half + 1))
                    if t.at_least(1):
                        dve.wait_ge(w_sb, t.n)
                    v_.tensor_tensor(w_pick[:], xb[t.par][:, :, COL_W:COL_W + E],
                                     exb[t.par][:, COL_HOT:COL_HOT + E].unsqueeze(1).to_broadcast([P, SUB, E]),
                                     ALU.mult).then_inc(pick_sb, 1)
                    if t.at_least(DEEP):
                        dve.wait_ge(added, ADDED * (t.n - DEEP + 1))
                    v_.tensor_copy(tok[t.par][:], xb[t.par][:, :, COL_ID])
                    dve.wait_ge(pick_sb, t.n + 1)
                    v_.tensor_reduce(w_row[t.par][:], w_pick[:], AX, ALU.add).then_inc(w_sb, 1)

            split_weights(XFIRST)
            rows_low(XFIRST)
            experts(dve, expert_step, 2)


def kernel(**inputs):
    import concourse.bacc as bacc
    from concourse.bass_utils import run_bass_kernel_spmd

    def given(name):
        return np.asarray(inputs[name])

    ffn, att = "L0_ffn_", "L0_xattn_"
    consts, tables = constants()
    columns = [given(att + n)[:, None] for n in ("wq_b", "wk_b", "wv_b")]
    columns += [given(ffn + "norm_weight")[:, None], given(ffn + "sb1").reshape(HC, P).T]
    bias_row = np.concatenate([np.tile(given(n), SUB) for n in (att + "wc_b", ffn + "sb2")])
    hot = np.broadcast_to(np.eye(E, dtype=np.float32)[:, None, :], (E, P, E))
    extra = np.concatenate([given(ffn + "eb1").reshape(E, HC, P).transpose(0, 2, 1),
                            given(ffn + "eb2")[:, :, None], hot], axis=2)
    arrays = {
        "x": given("x").reshape(TOKENS, D),
        "ctx_in": given("ctx_1024").reshape(TOKENS, D),
        "wq": given(att + "wq_w"), "wk": given(att + "wk_w"), "wv": given(att + "wv_w"), "wc": given(att + "wc_w"),
        "vecs": np.concatenate(columns, axis=1),
        "bias_rows": np.broadcast_to(bias_row, (2, 2 * TILE)),
        "router": given(ffn + "router_w").T,
        "sw1": given(ffn + "sw1"), "sw2": given(ffn + "sw2"),
        "ew1": given(ffn + "ew1"), "ew2": given(ffn + "ew2"),
        "extra": extra, "consts": consts, "tables": tables,
    }
    arrays = {name: np.ascontiguousarray(a) for name, a in arrays.items()}
    nc = bacc.Bacc("TRN2", target_bir_lowering=False, num_devices=1)
    aps = {name: nc.dram_tensor(name, a.shape, mybir.dt.from_np(a.dtype), kind="ExternalInput").ap()
           for name, a in arrays.items()}
    rows_dram = nc.dram_tensor("rows_dram", (X_ROWS, ROW), F32, kind="Internal").ap()
    out = nc.dram_tensor("out", (OUT_ROWS, D), F32, kind="ExternalOutput").ap()
    token_kernel(nc, **aps, rows_dram=rows_dram, out=out)
    result = run_bass_kernel_spmd(nc, [arrays], core_ids=[0]).results[0]["out"]
    return result[:TOKENS].reshape(128, 64, D)
```
